# Optimizing a Trainium2 kernel written in Bass

```python
import numpy as np
import jax
import jax.numpy as jnp

def _softmax(x, axis=-1):
    return jax.nn.softmax(x, axis=axis)

def _gelu(x):
    return jax.nn.gelu(x, approximate=True)

def _silu(x):
    return jax.nn.silu(x)

def _sigmoid(x):
    return jax.nn.sigmoid(x)

def _layernorm(x, axis=-1, eps=1e-05):
    m = jnp.mean(x, axis=axis, keepdims=True)
    v = jnp.var(x, axis=axis, keepdims=True)
    return (x - m) / jnp.sqrt(v + eps)

def _scatter_add(tgt, idx, src, axis=0):
    return tgt.at[idx].add(src)

def _segment_sum(src, seg, n):
    return jax.ops.segment_sum(src, seg, n)
kernel_name = 'mk_flamingo_gated_d1_seqx_r8_e5e71d'

def setup_inputs(seed: int=0):
    np.random.seed(seed)
    _w = jnp.asarray

    def _rec_inputs():
        import jax
        import jax.numpy as jnp
        _rk = jax.random.key(seed)
        x = 2.818e-05 + 1 * jax.random.normal(jax.random.fold_in(_rk, 1), (32, 128, 128), jnp.float32)
        _lenS = 128 - jax.random.randint(jax.random.fold_in(_rk, 7), (32,), 0, max(1, 128 // 4) + 1, jnp.int32)
        _lenS2 = 128 - jax.random.randint(jax.random.fold_in(_rk, 8), (32,), 0, max(1, 128 // 4) + 1, jnp.int32)
        _ctx_2048P = jax.random.normal(jax.random.fold_in(_rk, 11), (32, 16, 256), jnp.float32)
        _ctx_2048c = jax.random.dirichlet(jax.random.fold_in(_rk, 511), 0.3 * jnp.ones((16,), jnp.float32), (32, 128))
        _ctx_2048t = jnp.einsum('bsk,bkd->bsd', _ctx_2048c, _ctx_2048P)
        _ctx_2048t = _ctx_2048t * jax.lax.rsqrt(jnp.mean(jnp.square(_ctx_2048t)) + 1e-12) * 0.953939
        ctx_2048 = -0.000125008 + 0.999885 * (_ctx_2048t + 0.3 * jax.random.normal(jax.random.fold_in(_rk, 611), (32, 128, 256), jnp.float32))
        _validS = jnp.arange(128)[None, :] < _lenS[:, None]
        _validS2 = jnp.arange(128)[None, :] < _lenS2[:, None]
        _causal = jnp.tril(jnp.ones((128, 128), dtype=bool))
        mask_BxS2_fk1 = jnp.where(jnp.broadcast_to(_validS2[:, :], (32, 128)), 1.0, 0.0).astype(jnp.float32)
        _g = jax.random.normal(jax.random.fold_in(_rk, 9001), (2, 1), jnp.float32)
        _g = jnp.sign(_g) * jnp.maximum(jnp.abs(_g), 1.0) + (_g == 0) * 1.0
        g_xattn = _g[0]
        g_ffn = _g[1]
        return (x, ctx_2048, mask_BxS2_fk1, g_xattn, g_ffn)
    x, ctx_2048, mask_BxS2_fk1, g_xattn, g_ffn = _rec_inputs()

    def _L0_xattn_setup():
        import jax, jax.numpy as jnp
        import numpy as np
        B, S, T = (32, 64, 64)
        SRC_SIZE, TGT_SIZE, OUT_SIZE, NUM_HEAD = (256, 128, 128, 8)
        HEAD_DIM = OUT_SIZE // NUM_HEAD
        key = jax.random.key(seed)
        ks = jax.random.split(key, 12)
        src = jax.random.normal(ks[0], (B, S, SRC_SIZE), dtype=jnp.float32)
        tgt = jax.random.normal(ks[1], (B, T, TGT_SIZE), dtype=jnp.float32)
        src_mask = (jax.random.uniform(ks[2], (B, S)) > 0.3).astype(jnp.float32)
        src_mask = src_mask.at[:, 0].set(1.0)
        tgt_mask = (jax.random.uniform(ks[3], (B, T)) > 0.3).astype(jnp.float32)
        tgt_mask = tgt_mask.at[:, 0].set(1.0)

        def lin(k, out_f, in_f):
            return jax.random.normal(k, (out_f, in_f), dtype=jnp.float32) / np.sqrt(in_f)
        W_src = lin(ks[4], 2 * OUT_SIZE, SRC_SIZE)
        b_src = jnp.zeros((2 * OUT_SIZE,), jnp.float32)
        W_tgt = lin(ks[5], OUT_SIZE, TGT_SIZE)
        b_tgt = jnp.zeros((OUT_SIZE,), jnp.float32)
        W_out = lin(ks[6], OUT_SIZE, OUT_SIZE + TGT_SIZE)
        b_out = jnp.zeros((OUT_SIZE,), jnp.float32)
        return {'src': src, 'tgt': tgt, 'src_mask': src_mask, 'tgt_mask': tgt_mask, 'W_src': W_src, 'b_src': b_src, 'W_tgt': W_tgt, 'b_tgt': b_tgt, 'W_out': W_out, 'b_out': b_out}
    _L0_xattn_all = _L0_xattn_setup()
    _L0_xattn_in = {k: v for k, v in _L0_xattn_all.items() if k in ('W_src', 'b_src', 'W_tgt', 'b_tgt', 'W_out', 'b_out')}
    del _L0_xattn_all

    def _L0_ffn_setup():
        import jax, jax.numpy as jnp
        import numpy as np
        B, S, D, H, E = (2, 256, 128, 512, 8)
        key = jax.random.key(seed)
        k0, k1, k2, k3 = jax.random.split(key, 4)
        x = jax.random.normal(k0, (B, S, D), dtype=jnp.float32)
        router_w = jax.random.normal(k1, (E, D), dtype=jnp.float32) * 0.02
        w1 = jax.random.normal(k2, (E, D, H), dtype=jnp.float32) * 0.02
        w2 = jax.random.normal(k3, (E, H, D), dtype=jnp.float32) * 0.02
        return {'x': x, 'router_w': router_w, 'w1': w1, 'w2': w2}
    _L0_ffn_all = _L0_ffn_setup()
    _L0_ffn_in = {k: v for k, v in _L0_ffn_all.items() if k in ('router_w', 'w1', 'w2')}
    del _L0_ffn_all
    return {'x': x, 'ctx_2048': ctx_2048, 'mask_BxS2_fk1': mask_BxS2_fk1, 'g_xattn': g_xattn, 'g_ffn': g_ffn, 'L0_xattn_W_src': _L0_xattn_in['W_src'], 'L0_xattn_b_src': _L0_xattn_in['b_src'], 'L0_xattn_W_tgt': _L0_xattn_in['W_tgt'], 'L0_xattn_b_tgt': _L0_xattn_in['b_tgt'], 'L0_xattn_W_out': _L0_xattn_in['W_out'], 'L0_xattn_b_out': _L0_xattn_in['b_out'], 'L0_ffn_router_w': _L0_ffn_in['router_w'], 'L0_ffn_w1': _L0_ffn_in['w1'], 'L0_ffn_w2': _L0_ffn_in['w2']}

def reference(x, ctx_2048, mask_BxS2_fk1, g_xattn, g_ffn, L0_xattn_W_src, L0_xattn_b_src, L0_xattn_W_tgt, L0_xattn_b_tgt, L0_xattn_W_out, L0_xattn_b_out, L0_ffn_router_w, L0_ffn_w1, L0_ffn_w2):
    import jax
    import jax.numpy as jnp

    def _L0_xattn_ref(src, tgt, src_mask, tgt_mask, W_src, b_src, W_tgt, b_tgt, W_out, b_out):
        import jax, jax.numpy as jnp
        import numpy as np
        B, S, T = (32, 64, 64)
        SRC_SIZE, TGT_SIZE, OUT_SIZE, NUM_HEAD = (256, 128, 128, 8)
        HEAD_DIM = OUT_SIZE // NUM_HEAD
        b, s, _ = src.shape
        t = tgt.shape[1]
        src_trans = jnp.einsum('bsf,of->bso', src, W_src) + b_src
        tgt_trans = jnp.einsum('btf,of->bto', tgt, W_tgt) + b_tgt
        src_trans = src_trans * src_mask[:, :, None]
        tgt_trans = tgt_trans * tgt_mask[:, :, None]
        src_key, src_val = jnp.split(src_trans, 2, axis=2)
        k = src_key.reshape(b, s, NUM_HEAD, HEAD_DIM)
        v = src_val.reshape(b, s, NUM_HEAD, HEAD_DIM)
        q = tgt_trans.reshape(b, t, NUM_HEAD, HEAD_DIM)
        scores = jnp.einsum('bthd,bshd->bhts', q, k) / np.sqrt(HEAD_DIM)
        scores = jnp.where(src_mask[:, None, None, :] == 0, -jnp.inf, scores)
        attn = jax.nn.softmax(scores, axis=-1)
        tgt_update = jnp.einsum('bhts,bshd->bthd', attn, v).reshape(b, t, OUT_SIZE)
        cat_tgt = jnp.concatenate([tgt, tgt_update], axis=2)
        return jnp.einsum('btf,of->bto', cat_tgt, W_out) + b_out

    def _L0_ffn_ref(x, router_w, w1, w2):
        import jax, jax.numpy as jnp
        import numpy as np
        B, S, D, H, E = (2, 256, 128, 512, 8)
        b, s, d = x.shape
        e = router_w.shape[0]
        xf = x.reshape(-1, d)
        probs = jax.nn.softmax(xf @ router_w.T, axis=-1)
        topv, topi = jax.lax.top_k(probs, 2)
        topv = topv / (topv.sum(axis=-1, keepdims=True) + 1e-09)
        cw = (jax.nn.one_hot(topi, e, dtype=xf.dtype) * topv[..., None]).sum(axis=1)
        h = jax.nn.gelu(jnp.einsum('td,edh->teh', xf, w1), approximate=False)
        y = jnp.einsum('teh,ehd->ted', h, w2)
        out = jnp.einsum('te,ted->td', cw, y)
        return out.reshape(b, s, d)
    x = x + jnp.tanh(g_xattn[0]) * _L0_xattn_ref(ctx_2048, _layernorm(x, axis=-1), mask_BxS2_fk1, mask_BxS2_fk1, L0_xattn_W_src, L0_xattn_b_src, L0_xattn_W_tgt, L0_xattn_b_tgt, L0_xattn_W_out, L0_xattn_b_out)
    x = x + jnp.tanh(g_ffn[0]) * _L0_ffn_ref(_layernorm(x, axis=-1), L0_ffn_router_w, L0_ffn_w1, L0_ffn_w2)
    return x

_drawn_inputs = setup_inputs


def setup_inputs(seed=0):
    import zlib

    import numpy as np

    out = dict(_drawn_inputs(seed))
    spreads = {'L0_xattn_b_src': (0.0, 0.1), 'L0_xattn_b_tgt': (0.0, 0.769), 'L0_xattn_b_out': (0.0, 0.1)}
    factors = {}
    for name, (base, spread) in spreads.items():
        noise = np.random.default_rng([zlib.crc32(name.encode()), seed]).standard_normal(out[name].shape)
        drawn = base * np.exp(spread * noise) if base else spread * noise
        out[name] = jnp.asarray(drawn.astype(out[name].dtype))
    for name, factor in factors.items():
        out[name] = (out[name] * factor).astype(out[name].dtype)
    return out
```

```python
from contextlib import ExitStack

import concourse.bass as bass
from concourse import mybir

F32 = mybir.dt.float32
BF16 = mybir.dt.bfloat16
U32 = mybir.dt.uint32
ALU = mybir.AluOpType
ACT = mybir.ActivationFunctionType
AX = mybir.AxisListType

BATCH = 32
T = 128
D = 128
SRC = 256
FCH = SRC // 128
HEADS = 8
HD = D // HEADS
HALF = HEADS // 2
VPAD = 32
EXPERTS = 8
HID = 512
HCH = HID // 128
GROUP = 4
GROUPS = BATCH // GROUP
EPS = 1e-5
SCALE = float(HD) ** -0.5
MASKED = 1e30

LAG_PROJ = 4
LAG_SCORE = 6
LAG_PV = 7
LAG_O = 8
LAG_OUT = 3
LAG_ROUTE = 4
STEADY = 4
DRAINED = GROUPS + LAG_ROUTE


def each_step(eng, body):
    for g in range(STEADY):
        for k in range(GROUP):
            body(g, k)
    with eng.Fori(STEADY, GROUPS) as g:
        for k in range(GROUP):
            body(g, k)
    for g in range(GROUPS, DRAINED):
        for k in range(GROUP):
            body(g, k)


def sequence(g, k, lag):
    n = GROUP * g + (k - lag)
    if isinstance(n, int) and not 0 <= n < BATCH:
        return None
    return n


def group(g, lag):
    n = g - lag
    if isinstance(n, int) and not 0 <= n < GROUPS:
        return None
    return n


def wait(eng, sem, value):
    if not isinstance(value, int) or value > 0:
        eng.wait_ge(sem, value)


def gated_cross_attention_moe(nc, x, ctxT, mask, g_xattn, g_ffn, w_srcT, b_src, w_tgtT, b_tgt,
                              w_outT, b_out, routerT, w1, w2, ident_c, headmask_c, iota8_c, out):
    with ExitStack() as stack:
        def sb(name, shape, dt=F32):
            return stack.enter_context(nc.sbuf_tensor(name, shape, dt))

        def bank(name, cols=512):
            return stack.enter_context(nc.psum_tensor(name, [128, cols], F32))

        def sem(name):
            return stack.enter_context(nc.semaphore(name))

        ident = sb("ident", [128, 128])
        headmask = sb("headmask", [128, HEADS])
        iota8 = sb("iota8", [128, EXPERTS])
        wsrc = sb("wsrc", [128, FCH, SRC])
        wtgt = sb("wtgt", [128, D])
        wout = sb("wout", [128, 2, D])
        wout_g = sb("wout_g", [128, 2, D])
        bkey = sb("bkey", [128, 1])
        bqry = sb("bqry", [128, 1])
        bval = sb("bval", [128, D])
        bout = sb("bout", [128, D])
        bout_g = sb("bout_g", [128, D])
        gates = sb("gates", [128, 2])
        tgates = sb("tgates", [128, 2])
        router = sb("router", [128, 128])
        w1s = sb("w1s", [128, EXPERTS, HID])
        w2s = sb("w2s", [128, EXPERTS, HCH, D])
        maskbc = sb("maskbc", [128, BATCH * T])
        maskrow = sb("maskrow", [1, BATCH * T])
        penalty = sb("penalty", [128, BATCH * T], BF16)
        onesrow = sb("onesrow", [128, 128], BF16)
        scratch = sb("scratch", [128, 32])
        minus_half = sb("minus_half", [128, GROUP])
        xs = sb("xs", [128, BATCH, D])
        ctxs = sb("ctxs", [128, GROUP, FCH, T])
        xc = sb("xc", [128, GROUP, D])
        xn = sb("xn", [128, GROUP, D])
        x2c = sb("x2c", [128, GROUP, D])
        xnT = sb("xnT", [128, 2, T])
        kT = sb("kT", [128, 2, T])
        qT = sb("qT", [128, 2, T])
        kblk = sb("kblk", [128, 2, HEADS, T])
        vals = sb("vals", [128, 4, HEADS, VPAD])
        prob = sb("prob", [128, 2, HEADS, T])
        probT = sb("probT", [128, 2, HEADS, T])
        rowmax = sb("rowmax", [128, 2, HEADS])
        oT = sb("oT", [128, 2, T])
        rsum = sb("rsum", [128, 2, HEADS])
        on = sb("on", [128, GROUP, D])
        onT = sb("onT", [128, GROUP, T])
        st1 = sb("st1", [128, GROUP, 6])
        mv1 = sb("mv1", [128, GROUP, 2])
        ve1 = sb("ve1", [128, GROUP])
        nm1 = sb("nm1", [128, GROUP])
        rs1 = sb("rs1", [128, GROUP])
        st2 = sb("st2", [128, GROUP, 6])
        mv2 = sb("mv2", [128, GROUP, 2])
        ve2 = sb("ve2", [128, GROUP])
        nm2 = sb("nm2", [128, GROUP])
        rs2 = sb("rs2", [128, GROUP])
        x2n = sb("x2n", [128, GROUP, D])
        x2nT = sb("x2nT", [128, GROUP, T])
        x2nT_all = sb("x2nT_all", [128, BATCH, T])
        lmax = sb("lmax", [128, GROUP])
        lcen = sb("lcen", [128, GROUP, EXPERTS])
        lexp = sb("lexp", [128, GROUP, EXPERTS])
        lsum = sb("lsum", [128, GROUP])
        linv = sb("linv", [128, GROUP])
        rprob = sb("rprob", [128, GROUP, EXPERTS])
        top = sb("top", [128, GROUP, 8])
        topi = sb("topi", [128, GROUP, 8], U32)
        topf = sb("topf", [128, GROUP, 8])
        tsum = sb("tsum", [128, GROUP])
        tinv = sb("tinv", [128, GROUP])
        sel1 = sb("sel1", [128, GROUP, EXPERTS])
        sel2 = sb("sel2", [128, GROUP, EXPERTS])
        sel = sb("sel", [128, GROUP, EXPERTS])
        pw = sb("pw", [128, GROUP, EXPERTS])
        cw = sb("cw", [128, BATCH, EXPERTS])
        hid = sb("hid", [128, 2, HCH, GROUP * T])

        ps_score = [bank("ps_score0"), bank("ps_score1")]
        ps_pT = [bank("ps_pT0"), bank("ps_pT1")]
        ps_xT = bank("ps_xT")
        ps_proj = bank("ps_proj")
        ps_o = bank("ps_o")
        ps_tail = bank("ps_tail")

        s_const = sem("s_const")
        s_ffnw = sem("s_ffnw")
        s_x = sem("s_x")
        s_ctx = [sem(f"s_ctx{i}") for i in range(GROUP)]
        s_zero = sem("s_zero")
        s_pool0 = sem("s_pool0")
        s_gate = sem("s_gate")
        s_setup = sem("s_setup")
        s_st1 = sem("s_st1")
        s_nm1 = sem("s_nm1")
        s_ln1 = sem("s_ln1")
        s_rs1 = sem("s_rs1")
        s_xc = sem("s_xc")
        s_xn = sem("s_xn")
        s_xb = sem("s_xb")
        s_xT = sem("s_xT")
        s_xnT = sem("s_xnT")
        s_proj = sem("s_proj")
        s_k = sem("s_k")
        s_q = sem("s_q")
        s_v = sem("s_v")
        s_xo = sem("s_xo")
        s_kb = sem("s_kb")
        s_sc = sem("s_sc")
        s_max = sem("s_max")
        s_cen = sem("s_cen")
        s_exp = sem("s_exp")
        s_pT = sem("s_pT")
        s_pTs = sem("s_pTs")
        s_pv = sem("s_pv")
        s_oT = sem("s_oT")
        s_o = sem("s_o")
        s_rsum = sem("s_rsum")
        s_on = sem("s_on")
        s_onTp = sem("s_onTp")
        s_onT = sem("s_onT")
        s_oproj = sem("s_oproj")
        s_x2 = sem("s_x2")
        s_st2 = sem("s_st2")
        s_nm2 = sem("s_nm2")
        s_ln2 = sem("s_ln2")
        s_rs2 = sem("s_rs2")
        s_x2c = sem("s_x2c")
        s_x2n = sem("s_x2n")
        s_x2Tp = sem("s_x2Tp")
        s_x2nT = sem("s_x2nT")
        s_x2all = sem("s_x2all")
        s_lg = sem("s_lg")
        s_rt = sem("s_rt")
        s_lexp = sem("s_lexp")
        s_up = sem("s_up")
        s_gelu = sem("s_gelu")
        s_down = sem("s_down")
        s_acc = sem("s_acc")
        s_out = sem("s_out")

        ROUTE = 24
        STATS = 2 * GROUP

        x_v = x.rearrange("b t d -> t b d")
        out_v = out.rearrange("b t d -> t b d")
        mask_v = mask.rearrange("b t -> (b t)").unsqueeze(0)
        small = ((ident[:, :], ident_c), (headmask[:, :], headmask_c), (wtgt[:, :], w_tgtT),
                 (wsrc[:, :, :], w_srcT.rearrange("(c p) o -> p c o", p=128)),
                 (bkey[:, :], b_src[0:D].unsqueeze(1)),
                 (bqry[:, :], b_tgt.unsqueeze(1)),
                 (bval[:, :], b_src[D:2 * D].unsqueeze(0).broadcast_to([128, D])),
                 (bout[:, :], b_out.unsqueeze(0).broadcast_to([128, D])),
                 (gates[:, 0:1], g_xattn.unsqueeze(0).broadcast_to([128, 1])),
                 (gates[:, 1:2], g_ffn.unsqueeze(0).broadcast_to([128, 1])),
                 (wout[:, :, :], w_outT.rearrange("(c p) o -> p c o", p=128)),
                 (router[:, :], routerT),
                 (iota8[:, :], iota8_c),
                 (maskrow[:, :], mask_v),
                 (maskbc[:, :], mask_v.broadcast_to([128, BATCH * T])))
        ALL_CONST = 16 * len(small)

        def flat(ap):
            return ap.rearrange("p a b -> p (a b)")

        def heads(ap):
            return ap.rearrange("p (h s) -> p h s", h=HALF)

        def seqs(ap):
            return ap.rearrange("p (b s) -> p b s", b=GROUP)

        block = stack.enter_context(nc.Block())

        @block.sync
        def _(sp):
            sp.dma_start(xs[:, 0:GROUP, :], x_v[:, 0:GROUP, :]).then_inc(s_x, 16)
            for dst, src in small:
                sp.dma_start(dst, src).then_inc(s_const, 16)
            for b in range(GROUP):
                sp.dma_start(ctxs[:, b, :, :], ctxT[:, b, :, :]).then_inc(s_ctx[b], 16)
            with sp.Fori(1, GROUPS) as g:
                sp.wait_ge(s_x, 16 * g)
                sp.dma_start(xs[:, bass.ds(GROUP * g, GROUP), :],
                             x_v[:, bass.ds(GROUP * g, GROUP), :]).then_inc(s_x, 16)
                for b in range(GROUP):
                    sp.wait_ge(s_proj, GROUP * g + (b - GROUP + 1))
                    sp.dma_start(ctxs[:, b, :, :],
                                 ctxT[:, bass.ds(GROUP * g + b, 1), :, :]
                                 .rearrange("p o c t -> p (o c) t")).then_inc(s_ctx[b], 16)
            sp.dma_start(w1s[:, :, :], w1.rearrange("e d h -> d e h")).then_inc(s_ffnw, 16)
            for e in range(EXPERTS):
                sp.dma_start(w2s[:, e, :, :], w2[e, :, :].rearrange("(c p) d -> p c d", p=128)
                             ).then_inc(s_ffnw, 16)
            with sp.Fori(0, GROUPS) as g:
                sp.wait_ge(s_acc, GROUP * EXPERTS * (g + 1))
                sp.dma_start(out_v[:, bass.ds(GROUP * g, GROUP), :],
                             xs[:, bass.ds(GROUP * g, GROUP), :]).then_inc(s_out, 16)
            sp.wait_ge(s_out, 16 * GROUPS)

        @block.gpsimd
        def _(pool):
            nc.gpsimd.memset(minus_half[:, :], -0.5).then_inc(s_zero, 1)
            nc.gpsimd.memset(onesrow[:, :], 0.0).then_inc(s_zero, 1)
            nc.gpsimd.memset(vals[:, :, :, :], 0.0).then_inc(s_zero, 1)
            nc.gpsimd.memset(penalty[:, :], 0.0).then_inc(s_zero, 1)
            pool.wait_ge(s_zero, 4)
            nc.gpsimd.memset(onesrow[0:1, :], 1.0).then_inc(s_pool0, 1)
            nc.gpsimd.memset(vals[:, :, :, HD:HD + 1], 1.0).then_inc(s_pool0, 1)

            def step(g, k):
                G = group(g, 0)
                if k == 1 and G is not None:
                    pool.wait_ge(s_nm1, G + 1)
                    pool.wait_ge(s_ln1, G + 1)
                    wait(pool, s_xn, G)
                    nc.gpsimd.tensor_tensor(rs1[:, :], ve1[:, :], minus_half[:, :],
                                            ALU.pow).then_inc(s_rs1, 1)
                    nc.gpsimd.tensor_tensor(
                        xc[:, :, :], xs[:, bass.ds(GROUP * G, GROUP), :],
                        nm1[:, :].unsqueeze(2).broadcast_to([128, GROUP, D]),
                        ALU.add).then_inc(s_xc, 1)
                if k == 3 and G is not None:
                    pool.wait_ge(s_rs1, G + 1)
                    pool.wait_ge(s_xc, G + 1)
                    wait(pool, s_xT, GROUP * G)
                    nc.gpsimd.tensor_tensor(
                        xn[:, :, :], xc[:, :, :],
                        rs1[:, :].unsqueeze(2).broadcast_to([128, GROUP, D]),
                        ALU.mult).then_inc(s_xn, 1)
                    nc.gpsimd.tensor_tensor(
                        xs[:, bass.ds(GROUP * G, GROUP), :], xs[:, bass.ds(GROUP * G, GROUP), :],
                        bout_g[:, :].unsqueeze(1).broadcast_to([128, GROUP, D]),
                        ALU.add).then_inc(s_xb, 1)
                G = group(g, LAG_OUT)
                if k == 2 and G is not None:
                    pool.wait_ge(s_nm2, G + 1)
                    pool.wait_ge(s_ln2, G + 1)
                    wait(pool, s_x2n, G)
                    nc.gpsimd.tensor_tensor(rs2[:, :], ve2[:, :], minus_half[:, :],
                                            ALU.pow).then_inc(s_rs2, 1)
                    nc.gpsimd.tensor_tensor(
                        x2c[:, :, :], xs[:, bass.ds(GROUP * G, GROUP), :],
                        nm2[:, :].unsqueeze(2).broadcast_to([128, GROUP, D]),
                        ALU.add).then_inc(s_x2c, 1)
                    pool.wait_ge(s_rs2, G + 1)
                    pool.wait_ge(s_x2c, G + 1)
                    wait(pool, s_x2Tp, G)
                    nc.gpsimd.tensor_tensor(
                        x2n[:, :, :], x2c[:, :, :],
                        rs2[:, :].unsqueeze(2).broadcast_to([128, GROUP, D]),
                        ALU.mult).then_inc(s_x2n, 1)
                G = group(g, LAG_ROUTE)
                if k == 0 and G is not None:
                    pool.wait_ge(s_x2nT, G + 1)
                    nc.gpsimd.tensor_copy(x2nT_all[:, bass.ds(GROUP * G, GROUP), :],
                                          x2nT[:, :, :]).then_inc(s_x2all, 1)
                n = sequence(g, k, LAG_PROJ)
                if n is not None:
                    r = (k - LAG_PROJ) % 2
                    pool.wait_ge(s_k, n + 1)
                    wait(pool, s_sc, 2 * (n - 1))
                    nc.gpsimd.tensor_tensor(
                        kblk[:, r, :, :], kT[:, r, :].unsqueeze(1).broadcast_to([128, HEADS, T]),
                        headmask[:, :].unsqueeze(2).broadcast_to([128, HEADS, T]),
                        ALU.mult).then_inc(s_kb, 1)

            pool.wait_ge(s_setup, 4)
            each_step(pool, step)

        @block.scalar
        def _(act):
            act.wait_ge(s_const, ALL_CONST)
            nc.scalar.activation(tgates[:, :], gates[:, :], ACT.Tanh).then_inc(s_gate, 1)

            def step(g, k):
                n = sequence(g, k, LAG_PROJ)
                if n is not None:
                    act.wait_ge(s_xT, n + 1)
                    wait(act, s_proj, n - 1)
                    nc.scalar.activation(xnT[:, (k - LAG_PROJ) % 2, :], ps_xT[:, 0:T],
                                         ACT.Copy).then_inc(s_xnT, 1)
                G = group(g, LAG_OUT)
                if k == 0 and G is not None:
                    act.wait_ge(s_onTp, G + 1)
                    wait(act, s_oproj, G)
                    nc.scalar.activation(flat(onT[:, :, :]), ps_tail[:, :], ACT.Copy).then_inc(s_onT, 1)
                if k == 3 and G is not None:
                    act.wait_ge(s_x2Tp, G + 1)
                    wait(act, s_lg, G)
                    wait(act, s_x2all, G)
                    nc.scalar.activation(flat(x2nT[:, :, :]), ps_tail[:, :],
                                         ACT.Copy).then_inc(s_x2nT, 1)
                n = sequence(g, k, LAG_PV)
                if n is not None:
                    r = (k - LAG_PV) % 2
                    wait(act, s_pv, n - 1)
                    for h in range(2):
                        act.wait_ge(s_pT, 2 * n + (h + 1))
                        nc.scalar.activation(flat(probT[:, r, HALF * h:HALF * (h + 1), :]),
                                             ps_pT[h][:, :], ACT.Copy).then_inc(s_pTs, 1)
                n = sequence(g, k, LAG_SCORE)
                if n is not None:
                    r = (k - LAG_SCORE) % 2
                    for h in range(2):
                        act.wait_ge(s_cen, 2 * n + (h + 1))
                        p = flat(prob[:, r, HALF * h:HALF * (h + 1), :])
                        nc.scalar.activation(p, p, ACT.Exp, scale=SCALE).then_inc(s_exp, 1)
                G = group(g, LAG_ROUTE)
                if k == 2 and G is not None:
                    act.wait_ge(s_rt, ROUTE * G + 2)
                    nc.scalar.activation(flat(lexp[:, :, :]), flat(lcen[:, :, :]),
                                         ACT.Exp).then_inc(s_lexp, 1)
                n = sequence(g, k, LAG_PV)
                if n is not None:
                    act.wait_ge(s_pv, n + 1)
                    wait(act, s_o, n)
                    nc.scalar.activation(flat(oT[:, :, :]), ps_o[:, 0:2 * T], ACT.Copy).then_inc(s_oT, 1)

            each_step(act, step)

            def gelus(j):
                for e in range(EXPERTS):
                    m = EXPERTS * j + e
                    wait(act, s_down, m - 1)
                    for c in range(HCH):
                        act.wait_ge(s_up, HCH * m + (c + 1))
                        nc.scalar.activation(hid[:, e % 2, c, :], ps_score[c % 2][:, :],
                                             ACT.Gelu).then_inc(s_gelu, 1)

            gelus(0)
            with act.Fori(1, GROUPS) as j:
                gelus(j)

        @block.vector
        def _(dve):
            dve.wait_ge(s_const, ALL_CONST)
            dve.wait_ge(s_zero, 4)
            nc.vector.tensor_scalar(penalty[0:1, :], maskrow[:, :], -1.0, MASKED,
                                    ALU.add, ALU.mult).then_inc(s_setup, 1)
            dve.wait_ge(s_gate, 1)
            nc.vector.tensor_scalar(flat(wout_g[:, :, :]), flat(wout[:, :, :]), tgates[:, 0:1], None,
                                    ALU.mult).then_inc(s_setup, 1)
            nc.vector.tensor_scalar(bout_g[:, :], bout[:, :], tgates[:, 0:1], None,
                                    ALU.mult).then_inc(s_setup, 1)
            dve.wait_ge(s_setup, 3)
            nc.vector.memset(rsum[:, :, :], 1.0).then_inc(s_setup, 1)

            carriers = []

            def settled():
                carriers.append(None)
                c = len(carriers) % 32
                nc.vector.memset(scratch[:, c:c + 1], 0.0)

            def statistics(G, s, st, mv, ve, nm, done, used):
                wait(dve, used, G)
                settled()
                for b in range(GROUP):
                    nc.vector.bn_stats(st[:, b, :], xs[:, bass.ds(GROUP * G + b, 1), :]
                                       .rearrange("p o d -> p (o d)")).then_inc(s, 1)
                dve.wait_ge(s, STATS * G + GROUP)
                settled()
                for b in range(GROUP):
                    nc.vector.bn_aggr(mv[:, b, :], st[:, b, :]).then_inc(s, 1)
                dve.wait_ge(s, STATS * G + STATS)
                nc.vector.tensor_scalar(nm[:, :], mv[:, :, 0], -1.0, None, ALU.mult).then_inc(done[0], 1)
                nc.vector.tensor_scalar(ve[:, :], mv[:, :, 1], EPS, None, ALU.add).then_inc(done[1], 1)

            def route(G):
                at = [0]

                def then(ins):
                    at[0] += 1
                    ins.then_inc(s_rt, 1)

                def done(back=0):
                    dve.wait_ge(s_rt, ROUTE * G + (at[0] - back))

                logits = seqs(ps_tail[:, :])[:, :, 0:EXPERTS]

                def per_expert(ap):
                    return ap.unsqueeze(2).broadcast_to([128, GROUP, EXPERTS])

                dve.wait_ge(s_lg, G + 1)
                then(nc.vector.tensor_reduce(lmax[:, :], logits, AX.X, ALU.max))
                done()
                then(nc.vector.tensor_tensor(lcen[:, :, :], logits, per_expert(lmax[:, :]),
                                             ALU.subtract))
                dve.wait_ge(s_lexp, G + 1)
                then(nc.vector.tensor_reduce(lsum[:, :], lexp[:, :, :], AX.X, ALU.add))
                done()
                then(nc.vector.reciprocal(linv[:, :], lsum[:, :]))
                done()
                then(nc.vector.tensor_tensor(rprob[:, :, :], lexp[:, :, :], per_expert(linv[:, :]),
                                             ALU.mult))
                done()
                settled()
                for b in range(GROUP):
                    then(nc.vector.max(top[:, b, :], rprob[:, b, :]))
                done()
                settled()
                for b in range(GROUP):
                    then(nc.vector.max_index(topi[:, b, :], top[:, b, :], rprob[:, b, :]))
                done()
                then(nc.vector.tensor_copy(topf[:, :, :], topi[:, :, :]))
                then(nc.vector.scalar_tensor_tensor(tsum[:, :], top[:, :, 0], 1e-9, top[:, :, 1],
                                                    ALU.add, ALU.add))
                done()
                experts = iota8[:, :].unsqueeze(1).broadcast_to([128, GROUP, EXPERTS])
                then(nc.vector.tensor_tensor(sel1[:, :, :], experts, per_expert(topf[:, :, 0]),
                                             ALU.is_equal))
                then(nc.vector.tensor_tensor(sel2[:, :, :], experts, per_expert(topf[:, :, 1]),
                                             ALU.is_equal))
                then(nc.vector.reciprocal(tinv[:, :], tsum[:, :]))
                done()
                then(nc.vector.tensor_tensor(sel[:, :, :], sel1[:, :, :], sel2[:, :, :], ALU.add))
                then(nc.vector.tensor_scalar(tinv[:, :], tinv[:, :], tgates[:, 1:2], None, ALU.mult))
                done()
                then(nc.vector.tensor_tensor(pw[:, :, :], rprob[:, :, :], sel[:, :, :], ALU.mult))
                done()
                then(nc.vector.tensor_tensor(cw[:, bass.ds(GROUP * G, GROUP), :], pw[:, :, :],
                                             per_expert(tinv[:, :]), ALU.mult))
                done()
                while at[0] < ROUTE:
                    then(nc.vector.memset(lsum[:, :], 0.0))
                    done()

            def step(g, k):
                n = sequence(g, k, LAG_SCORE)
                if n is not None:
                    r = (k - LAG_SCORE) % 2
                    wait(dve, s_cen, 2 * (n - 1))
                    for h in range(2):
                        dve.wait_ge(s_sc, 2 * n + (h + 1))
                        nc.vector.tensor_reduce(rowmax[:, r, HALF * h:HALF * (h + 1)],
                                                heads(ps_score[h][:, :]), AX.X, ALU.max
                                                ).then_inc(s_max, 1)
                    wait(dve, s_pT, 2 * (n - 1))
                    for h in range(2):
                        dve.wait_ge(s_max, 2 * n + (h + 1))
                        nc.vector.tensor_tensor(
                            prob[:, r, HALF * h:HALF * (h + 1), :], heads(ps_score[h][:, :]),
                            rowmax[:, r, HALF * h:HALF * (h + 1)].unsqueeze(2)
                            .broadcast_to([128, HALF, T]), ALU.subtract).then_inc(s_cen, 1)
                n = sequence(g, k, LAG_O)
                if n is not None:
                    r = (k - LAG_O) % 2
                    o3 = ps_o[:, 0:2 * T].rearrange("p (h c) -> p h c", c=VPAD)
                    dve.wait_ge(s_o, n + 1)
                    wait(dve, s_on, n - 1)
                    nc.vector.reciprocal(rsum[:, r, :], o3[:, :, HD]).then_inc(s_rsum, 1)
                    dve.wait_ge(s_rsum, n + 1)
                    wait(dve, s_onTp, g - LAG_O // GROUP)
                    nc.vector.tensor_tensor(
                        on[:, (k - LAG_O) % GROUP, :].rearrange("p (h c) -> p h c", c=HD),
                        o3[:, :, 0:HD], rsum[:, r, :].unsqueeze(2).broadcast_to([128, HEADS, HD]),
                        ALU.mult).then_inc(s_on, 1)
                n = sequence(g, k, LAG_PROJ)
                if n is not None:
                    r = (k - LAG_PROJ) % 2
                    cols = bass.ds(n * T, T)
                    dve.wait_ge(s_proj, n + 1)
                    wait(dve, s_kb, n - 1)
                    nc.vector.scalar_tensor_tensor(kT[:, r, :], ps_proj[:, 0:T], bkey[:, :],
                                                   maskbc[:, cols], ALU.add, ALU.mult).then_inc(s_k, 1)
                    wait(dve, s_sc, 2 * (n - 1))
                    nc.vector.scalar_tensor_tensor(qT[:, r, :], ps_proj[:, T:2 * T], bqry[:, :],
                                                   maskbc[:, cols], ALU.add, ALU.mult).then_inc(s_q, 1)
                    wait(dve, s_pv, n - 3)
                    nc.vector.tensor_tensor(
                        vals[:, (k - LAG_PROJ) % 4, :, 0:HD],
                        ps_proj[:, 2 * T:3 * T].rearrange("p (h c) -> p h c", c=HD),
                        bval[:, :].rearrange("p (h c) -> p h c", c=HD), ALU.add).then_inc(s_v, 1)
                    dve.wait_ge(s_xb, g)
                    x1 = xs[:, bass.ds(n, 1), :].rearrange("p o d -> p (o d)")
                    nc.vector.tensor_tensor(x1, ps_proj[:, 3 * T:4 * T], x1, ALU.add).then_inc(s_xo, 1)
                G = group(g, 0)
                if k == 0 and G is not None:
                    dve.wait_ge(s_x, 16 * (G + 1))
                    statistics(G, s_st1, st1, mv1, ve1, nm1, (s_nm1, s_ln1), s_xc)
                G = group(g, LAG_OUT)
                if k == 1 and G is not None:
                    dve.wait_ge(s_oproj, G + 1)
                    wait(dve, s_xo, GROUP * G + GROUP)
                    x4 = xs[:, bass.ds(GROUP * G, GROUP), :]
                    nc.vector.tensor_tensor(x4, seqs(ps_tail[:, :]), x4, ALU.add).then_inc(s_x2, 1)
                    dve.wait_ge(s_x2, G + 1)
                    statistics(G, s_st2, st2, mv2, ve2, nm2, (s_nm2, s_ln2), s_x2c)
                G = group(g, LAG_ROUTE)
                if k == 2 and G is not None:
                    route(G)

            each_step(dve, step)

            def accumulate(j):
                for e in range(EXPERTS):
                    m = EXPERTS * j + e
                    dve.wait_ge(s_down, m + 1)
                    for b in range(GROUP):
                        n = GROUP * j + b
                        wait(dve, s_acc, GROUP * m + (b + 1 - GROUP))
                        x1 = xs[:, bass.ds(n, 1), :].rearrange("p o d -> p (o d)")
                        nc.vector.scalar_tensor_tensor(
                            x1, ps_pT[e % 2][:, b * D:(b + 1) * D],
                            cw[:, bass.ds(n, 1), e:e + 1].rearrange("p o e -> p (o e)"), x1,
                            ALU.mult, ALU.add).then_inc(s_acc, 1)

            accumulate(0)
            with dve.Fori(1, GROUPS) as j:
                accumulate(j)

        @block.tensor
        def _(pe):
            pe.wait_ge(s_const, ALL_CONST)
            pe.wait_ge(s_pool0, 2)
            pe.wait_ge(s_setup, 4)

            def step(g, k):
                n = sequence(g, k, LAG_PROJ)
                if n is not None:
                    wait(pe, s_xn, g)
                    wait(pe, s_xnT, n)
                    nc.tensor.transpose(ps_xT[:, 0:T], xn[:, (k - LAG_PROJ) % GROUP, :],
                                        ident[:, :]).then_inc(s_xT, 1)
                G = group(g, LAG_OUT)
                if k == 0 and G is not None:
                    pe.wait_ge(s_on, GROUP * G + GROUP)
                    wait(pe, s_x2nT, G)
                    for b in range(GROUP):
                        last = nc.tensor.transpose(ps_tail[:, b * T:(b + 1) * T], on[:, b, :], ident[:, :])
                    last.then_inc(s_onTp, 1)
                if k == 1 and G is not None:
                    pe.wait_ge(s_onT, G + 1)
                    for b in range(GROUP):
                        last = nc.tensor.matmul(ps_tail[:, b * D:(b + 1) * D], onT[:, b, :],
                                                wout_g[:, 1, :], start=True, stop=True)
                    last.then_inc(s_oproj, 1)
                if k == 3 and G is not None:
                    pe.wait_ge(s_x2n, G + 1)
                    wait(pe, s_rt, ROUTE * (G - 1) + 2)
                    for b in range(GROUP):
                        last = nc.tensor.transpose(ps_tail[:, b * T:(b + 1) * T], x2n[:, b, :], ident[:, :])
                    last.then_inc(s_x2Tp, 1)
                G = group(g, LAG_ROUTE)
                if k == 2 and G is not None:
                    pe.wait_ge(s_x2nT, G + 1)
                    wait(pe, s_x2, min(G + 2, GROUPS) if isinstance(G, int) else G + 2)
                    for b in range(GROUP):
                        last = nc.tensor.matmul(ps_tail[:, b * 128:(b + 1) * 128], x2nT[:, b, :],
                                                router[:, :], start=True, stop=True)
                    last.then_inc(s_lg, 1)
                n = sequence(g, k, LAG_SCORE)
                if n is not None:
                    r = (k - LAG_SCORE) % 2
                    pe.wait_ge(s_q, n + 1)
                    pe.wait_ge(s_kb, n + 1)
                    for h in range(2):
                        wait(pe, s_cen, 2 * n + (h - 1))
                        nc.tensor.matmul(ps_score[h][:, :], qT[:, r, :],
                                         flat(kblk[:, r, HALF * h:HALF * (h + 1), :]),
                                         start=True, stop=False)
                        nc.tensor.matmul(ps_score[h][:, :], onesrow[:, :],
                                         penalty[:, bass.ds(n * T, T)].unsqueeze(1)
                                         .broadcast_to([128, HALF, T]),
                                         start=False, stop=True).then_inc(s_sc, 1)
                n = sequence(g, k, LAG_O)
                if n is not None:
                    pe.wait_ge(s_oT, n + 1)
                    for h in range(2):
                        last = nc.tensor.transpose(ps_o[:, h * T:(h + 1) * T], oT[:, h, :], ident[:, :])
                    last.then_inc(s_o, 1)
                n = sequence(g, k, LAG_PV)
                if n is not None:
                    r = (k - LAG_PV) % 2
                    for h in range(2):
                        pe.wait_ge(s_exp, 2 * n + (h + 1))
                        wait(pe, s_pTs, 2 * n + (h - 1))
                        for j in range(HALF):
                            last = nc.tensor.transpose(ps_pT[h][:, j * T:(j + 1) * T],
                                                       prob[:, r, HALF * h + j, :], ident[:, :])
                        last.then_inc(s_pT, 1)
                n = sequence(g, k, LAG_PROJ)
                if n is not None:
                    r = (k - LAG_PROJ) % 2
                    b = (k - LAG_PROJ) % GROUP
                    pe.wait_ge(s_xnT, n + 1)
                    pe.wait_ge(s_ctx[b], 16 * g)
                    wait(pe, s_xo, n)
                    for c in range(FCH):
                        nc.tensor.matmul(ps_proj[:, 0:T], wsrc[:, c, 0:D], ctxs[:, b, c, :],
                                         start=(c == 0), stop=(c == FCH - 1))
                    nc.tensor.matmul(ps_proj[:, T:2 * T], wtgt[:, :], xnT[:, r, :], start=True, stop=True)
                    for c in range(FCH):
                        nc.tensor.matmul(ps_proj[:, 2 * T:3 * T], ctxs[:, b, c, :], wsrc[:, c, D:2 * D],
                                         start=(c == 0), stop=(c == FCH - 1))
                    nc.tensor.matmul(ps_proj[:, 3 * T:4 * T], xnT[:, r, :], wout_g[:, 0, :],
                                     start=True, stop=True).then_inc(s_proj, 1)
                n = sequence(g, k, LAG_PV)
                if n is not None:
                    r = (k - LAG_PV) % 2
                    pe.wait_ge(s_pTs, 2 * n + 2)
                    pe.wait_ge(s_v, n + 1)
                    wait(pe, s_on, n)
                    for h in range(HEADS):
                        q = h % HALF
                        last = nc.tensor.matmul(
                            ps_o[VPAD * q:VPAD * (q + 1), (h // HALF) * T:(h // HALF + 1) * T],
                            vals[:, (k - LAG_PV) % 4, h, :], probT[:, r, h, :], start=True, stop=True)
                    last.then_inc(s_pv, 1)

            each_step(pe, step)

            pe.wait_ge(s_ffnw, 16 * (1 + EXPERTS))
            pe.wait_ge(s_x2all, GROUPS)
            pe.wait_ge(s_cen, 2 * BATCH)
            pe.wait_ge(s_pTs, 2 * BATCH)

            def down(m, e):
                pe.wait_ge(s_gelu, HCH * m + HCH)
                wait(pe, s_acc, GROUP * (m - 1))
                for b in range(GROUP):
                    for c in range(HCH):
                        last = nc.tensor.matmul(ps_pT[e % 2][:, b * D:(b + 1) * D],
                                                hid[:, e % 2, c, b * T:(b + 1) * T], w2s[:, e, c, :],
                                                start=(c == 0), stop=(c == HCH - 1))
                last.then_inc(s_down, 1)

            def experts(j, first):
                rows = flat(x2nT_all[:, bass.ds(GROUP * j, GROUP), :])
                for e in range(EXPERTS):
                    m = EXPERTS * j + e
                    for c in range(HCH):
                        wait(pe, s_gelu, HCH * m + (c - 1))
                        nc.tensor.matmul(ps_score[c % 2][:, :], w1s[:, e, c * 128:(c + 1) * 128],
                                         rows, start=True, stop=True).then_inc(s_up, 1)
                    if not (first and e == 0):
                        down(m - 1, (e - 1) % EXPERTS)

            experts(0, True)
            with pe.Fori(1, GROUPS) as j:
                experts(j, False)
            down(EXPERTS * GROUPS - 1, EXPERTS - 1)


def kernel(x, ctx_2048, mask_BxS2_fk1, g_xattn, g_ffn, L0_xattn_W_src, L0_xattn_b_src,
           L0_xattn_W_tgt, L0_xattn_b_tgt, L0_xattn_W_out, L0_xattn_b_out, L0_ffn_router_w,
           L0_ffn_w1, L0_ffn_w2):
    import numpy as np
    import concourse.bacc as bacc
    from concourse.bass_utils import run_bass_kernel_spmd

    router = np.zeros((128, 128), np.float32)
    router[:, :EXPERTS] = np.asarray(L0_ffn_router_w).T
    ctx = np.asarray(ctx_2048)
    arrays = {
        "x": x, "ctxT": ctx.transpose(2, 0, 1).reshape(FCH, 128, BATCH, T).transpose(1, 2, 0, 3),
        "mask": mask_BxS2_fk1, "g_xattn": g_xattn, "g_ffn": g_ffn,
        "w_srcT": np.asarray(L0_xattn_W_src).T, "b_src": L0_xattn_b_src,
        "w_tgtT": np.asarray(L0_xattn_W_tgt).T, "b_tgt": L0_xattn_b_tgt,
        "w_outT": np.asarray(L0_xattn_W_out).T, "b_out": L0_xattn_b_out,
        "routerT": router, "w1": L0_ffn_w1, "w2": L0_ffn_w2,
        "ident_c": np.eye(128, dtype=np.float32),
        "headmask_c": np.kron(np.eye(HEADS), np.ones((HD, 1))).astype(np.float32),
        "iota8_c": np.tile(np.arange(EXPERTS, dtype=np.float32), (128, 1)),
    }
    nc = bacc.Bacc("TRN2", target_bir_lowering=False, num_devices=1)
    arrays = {k: np.ascontiguousarray(a) for k, a in arrays.items()}
    args = {k: nc.dram_tensor(k, a.shape, mybir.dt.from_np(a.dtype), kind="ExternalInput").ap()
            for k, a in arrays.items()}
    out = nc.dram_tensor("out", [BATCH, T, D], F32, kind="ExternalOutput").ap()
    gated_cross_attention_moe(nc, out=out, **args)
    r = run_bass_kernel_spmd(nc, [arrays], core_ids=[0])
    return r.results[0]["out"]
```

```python
from contextlib import ExitStack

import concourse.bass as bass
from concourse import mybir

F32 = mybir.dt.float32
BF16 = mybir.dt.bfloat16
U32 = mybir.dt.uint32
I32 = mybir.dt.int32
F32R = mybir.dt.float32r
ALU = mybir.AluOpType
ACT = mybir.ActivationFunctionType
AX = mybir.AxisListType

BATCH = 32
T = 128
D = 128
SRC = 256
FCH = SRC // 128
HEADS = 8
HD = D // HEADS
HALF = HEADS // 2
VPAD = 32
EXPERTS = 8
HID = 512
HCH = HID // 128
GROUP = 4
GROUPS = BATCH // GROUP
EPS = 1e-5
SCALE = float(HD) ** -0.5
MASKED = 1e30

LAG_PROJ = 4
LAG_SCORE = 6
LAG_PV = 7
LAG_O = 8
LAG_OUT = 3
LAG_ROUTE = 4
LAG_SEND = 5
STEADY = LAG_SEND
DRAINED = GROUPS + LAG_SEND + 1

ROW = D + 2
CAP = BATCH * T
REGION = CAP + 128
PICKS = 2 * BATCH * T
RING = 8
SLOTS = -(-(PICKS // 128 + EXPERTS - 1) // RING) * RING
SPARE = SLOTS - PICKS // 128
NOWHERE = 1 << 20
W1_STEPS = range(GROUP, GROUP + EXPERTS)


def each_step(eng, body):
    for g in range(STEADY):
        for k in range(GROUP):
            body(g, k)
    with eng.Fori(STEADY, GROUPS) as g:
        for k in range(GROUP):
            body(g, k)
    for g in range(GROUPS, DRAINED):
        for k in range(GROUP):
            body(g, k)


def sequence(g, k, lag):
    n = GROUP * g + (k - lag)
    if isinstance(n, int) and not 0 <= n < BATCH:
        return None
    return n


def group(g, lag):
    n = g - lag
    if isinstance(n, int) and not 0 <= n < GROUPS:
        return None
    return n


def each_slot(eng, body):
    for r in range(RING):
        body(0, r)
    with eng.Fori(1, SLOTS // RING) as q:
        for r in range(RING):
            body(q, r)
    for r in range(3):
        body(SLOTS // RING, r)


def slot_of(q, r, lag):
    j = RING * q + (r - lag)
    if isinstance(j, int) and not 0 <= j < SLOTS:
        return None
    return j


def wait(eng, sem, value):
    if not isinstance(value, int) or value > 0:
        eng.wait_ge(sem, value)


def gated_cross_attention_moe(nc, x, ctxT, mask, g_xattn, g_ffn, w_srcT, b_src, w_tgtT, b_tgt,
                              w_outT, b_out, routerT, w1, w2, ident_c, headmask_c, iota_c, dest_c, strict_c,
                              below_c, padmeta_c, rows, picked, out):
    with ExitStack() as stack:
        def sb(name, shape, dt=F32):
            return stack.enter_context(nc.sbuf_tensor(name, shape, dt))

        def bank(name, cols=512):
            return stack.enter_context(nc.psum_tensor(name, [128, cols], F32))

        def sem(name):
            return stack.enter_context(nc.semaphore(name))

        ident = sb("ident", [128, 128])
        headmask = sb("headmask", [128, HEADS])
        iota = sb("iota", [128, SLOTS + EXPERTS])
        iota8 = iota[:, 0:EXPERTS]
        dest = sb("dest", [128, BATCH, 2], I32)
        strict = sb("strict", [128, 128])
        strict_b = sb("strict_b", [128, 128], BF16)
        ones_b = sb("ones_b", [128, 128], BF16)
        below = sb("below", [128, EXPERTS, EXPERTS])
        padrow = sb("padrow", [128, ROW])
        regions = sb("regions", [128, EXPERTS])
        wsrc = sb("wsrc", [128, FCH, SRC])
        wtgt = sb("wtgt", [128, D])
        wout = sb("wout", [128, 2, D])
        wout_g = sb("wout_g", [128, 2, D])
        bkey = sb("bkey", [128, 1])
        bqry = sb("bqry", [128, 1])
        bval = sb("bval", [128, D])
        bout = sb("bout", [128, D])
        bout_g = sb("bout_g", [128, D])
        gates = sb("gates", [128, 2])
        tgates = sb("tgates", [128, 2])
        router = sb("router", [128, 128])
        w1s = sb("w1s", [128, EXPERTS, HID])
        w2s = sb("w2s", [128, EXPERTS, HCH, D])
        maskbc = sb("maskbc", [128, BATCH * T])
        maskrow = sb("maskrow", [1, BATCH * T])
        penalty = sb("penalty", [128, BATCH * T], BF16)
        onesrow = sb("onesrow", [128, 128], BF16)
        scratch = sb("scratch", [128, 32])
        pscratch = sb("pscratch", [128, 32])
        minus_half = sb("minus_half", [128, GROUP])
        xs = sb("xs", [128, BATCH, D])
        ctxs = sb("ctxs", [128, GROUP, FCH, T])
        xn = sb("xn", [128, GROUP, D])
        xnT = sb("xnT", [128, 2, T])
        kT = sb("kT", [128, 2, T])
        qT = sb("qT", [128, 2, T])
        kblk = sb("kblk", [128, 2, HEADS, T])
        vals = sb("vals", [128, 4, HEADS, VPAD])
        prob = sb("prob", [128, 2, HEADS, T])
        probT = sb("probT", [128, 2, HEADS, T])
        rowmax = sb("rowmax", [128, 2, HEADS])
        oT = sb("oT", [128, 2, T])
        rsum = sb("rsum", [128, 2, HEADS])
        on = sb("on", [128, GROUP, D])
        onT = sb("onT", [128, GROUP, T])
        st1 = sb("st1", [128, GROUP, 6])
        mv1 = sb("mv1", [128, GROUP, 2])
        ve1 = sb("ve1", [128, GROUP])
        nm1 = sb("nm1", [128, GROUP])
        rs1 = sb("rs1", [128, GROUP])
        st2 = sb("st2", [128, GROUP, 6])
        mv2 = sb("mv2", [128, GROUP, 2])
        ve2 = sb("ve2", [128, GROUP])
        nm2 = sb("nm2", [128, GROUP])
        rs2 = sb("rs2", [128, GROUP])
        x2n = sb("x2n", [128, GROUP, D])
        x2nT = sb("x2nT", [128, GROUP, T])
        lmax = sb("lmax", [128, GROUP])
        lcen = sb("lcen", [128, GROUP, EXPERTS])
        lexp = sb("lexp", [128, GROUP, EXPERTS])
        lsum = sb("lsum", [128, GROUP])
        linv = sb("linv", [128, GROUP])
        rprob = sb("rprob", [128, GROUP, EXPERTS])
        top = sb("top", [128, GROUP, 8])
        topi = sb("topi", [128, GROUP, 8], U32)
        topf = sb("topf", [128, GROUP, 8])
        tsum = sb("tsum", [128, GROUP])
        tinv = sb("tinv", [128, GROUP])
        tw = sb("tw", [128, GROUP])
        sel = sb("sel", [128, 2, GROUP, EXPERTS])
        sel_b = sb("sel_b", [128, GROUP, EXPERTS], BF16)
        before = sb("before", [128, EXPERTS], BF16)
        picks = sb("picks", [128, EXPERTS])
        place = sb("place", [128, GROUP, EXPERTS])
        placed = sb("placed", [128, 2, GROUP, EXPERTS])
        pos = sb("pos", [128, 2, GROUP])
        posi = sb("posi", [128, 2, GROUP], I32)
        xr = sb("xr", [128, 2, GROUP, ROW])
        total = sb("total", [128, EXPERTS])
        more = sb("more", [128, EXPERTS, BATCH])
        nslots = sb("nslots", [128, EXPERTS])
        upto = sb("upto", [128, EXPERTS, EXPERTS])
        ends = sb("ends", [128, EXPERTS])
        past = sb("past", [128, SLOTS, EXPERTS])
        gone = sb("gone", [128, SLOTS, EXPERTS])
        sexp = sb("sexp", [128, SLOTS])
        sgone = sb("sgone", [128, SLOTS])
        srow = sb("srow", [128, SLOTS])
        slot_row = sb("slot_row", [128, SLOTS], I32)
        slot_exp = sb("slot_exp", [128, SLOTS], I32)
        prow = sb("prow", [128, EXPERTS])
        pad_row = sb("pad_row", [128, EXPERTS], I32)
        w1h = sb("w1h", [128, EXPERTS, HID], F32R)
        w1l = sb("w1l", [128, EXPERTS, HID], F32R)
        xg = sb("xg", [128, RING, ROW])
        xh = sb("xh", [128, 2, 128], F32R)
        xl = sb("xl", [128, 2, 128], F32R)
        yo = sb("yo", [128, RING, D])
        hid = probT[:, :, 0:HCH, :]
        hidT = probT[:, :, HCH:2 * HCH, :]
        yb = prob[:, :, :, :].rearrange("p r (b k) d -> p r b k d", k=2)

        ps_score = [bank("ps_score0"), bank("ps_score1")]
        ps_pT = [bank("ps_pT0"), bank("ps_pT1")]
        ps_xT = bank("ps_xT")
        ps_proj = bank("ps_proj")
        ps_o = bank("ps_o")
        ps_tail = bank("ps_tail")
        ps_y = [ps_proj, ps_o]

        s_const = sem("s_const")
        s_ffnw = sem("s_ffnw")
        s_x = sem("s_x")
        s_ctx = [sem(f"s_ctx{i}") for i in range(GROUP)]
        s_zero = sem("s_zero")
        s_pool0 = sem("s_pool0")
        s_gate = sem("s_gate")
        s_setup = sem("s_setup")
        s_st1 = sem("s_st1")
        s_nm1 = sem("s_nm1")
        s_ln1 = sem("s_ln1")
        s_rs1 = sem("s_rs1")
        s_xn = sem("s_xn")
        s_xb = sem("s_xb")
        s_xT = sem("s_xT")
        s_xnT = sem("s_xnT")
        s_proj = sem("s_proj")
        s_k = sem("s_k")
        s_q = sem("s_q")
        s_v = sem("s_v")
        s_xo = sem("s_xo")
        s_kb = sem("s_kb")
        s_sc = sem("s_sc")
        s_max = sem("s_max")
        s_cen = sem("s_cen")
        s_exp = sem("s_exp")
        s_pT = sem("s_pT")
        s_pTs = sem("s_pTs")
        s_pv = sem("s_pv")
        s_oT = sem("s_oT")
        s_o = sem("s_o")
        s_rsum = sem("s_rsum")
        s_on = sem("s_on")
        s_onTp = sem("s_onTp")
        s_onT = sem("s_onT")
        s_oproj = sem("s_oproj")
        s_x2 = sem("s_x2")
        s_st2 = sem("s_st2")
        s_nm2 = sem("s_nm2")
        s_ln2 = sem("s_ln2")
        s_rs2 = sem("s_rs2")
        s_x2n = sem("s_x2n")
        s_x2Tp = sem("s_x2Tp")
        s_x2nT = sem("s_x2nT")
        s_xr = sem("s_xr")
        s_lg = sem("s_lg")
        s_rt = sem("s_rt")
        s_lexp = sem("s_lexp")
        s_rank = sem("s_rank")
        s_pos = sem("s_pos")
        s_send = sem("s_send")
        s_pads = sem("s_pads")
        s_total = sem("s_total")
        s_plan = sem("s_plan")
        s_w1h = sem("s_w1h")
        s_w1l = sem("s_w1l")
        f_load = [sem(f"f_load{i}") for i in range(RING)]
        f_xT = sem("f_xT")
        f_xh = sem("f_xh")
        f_xl = sem("f_xl")
        f_up = sem("f_up")
        f_gelu = sem("f_gelu")
        f_hT = sem("f_hT")
        f_hTs = sem("f_hTs")
        f_down = sem("f_down")
        f_y = sem("f_y")
        f_send = [sem(f"f_send{i}") for i in range(RING)]
        f_settled = sem("f_settled")
        s_yb = [sem(f"s_yb{i}") for i in range(2)]
        s_y1 = sem("s_y1")
        s_y2 = sem("s_y2")
        s_out = sem("s_out")

        ROUTE = 23
        STATS = 2 * GROUP
        POS = 5
        SEND = 16 * 2 * GROUP
        PLAN = 16

        x_v = x.rearrange("b t d -> t b d")
        out_v = out.rearrange("b t d -> t b d")
        picked_v = picked.rearrange("(b t k) d -> t b k d", t=T, k=2)
        mask_v = mask.rearrange("b t -> (b t)").unsqueeze(0)
        small = ((ident[:, :], ident_c), (headmask[:, :], headmask_c), (wtgt[:, :], w_tgtT),
                 (wsrc[:, :, :], w_srcT.rearrange("(c p) o -> p c o", p=128)),
                 (bkey[:, :], b_src[0:D].unsqueeze(1)),
                 (bqry[:, :], b_tgt.unsqueeze(1)),
                 (bval[:, :], b_src[D:2 * D].unsqueeze(0).broadcast_to([128, D])),
                 (bout[:, :], b_out.unsqueeze(0).broadcast_to([128, D])),
                 (gates[:, 0:1], g_xattn.unsqueeze(0).broadcast_to([128, 1])),
                 (gates[:, 1:2], g_ffn.unsqueeze(0).broadcast_to([128, 1])),
                 (wout[:, :, :], w_outT.rearrange("(c p) o -> p c o", p=128)),
                 (router[:, :], routerT),
                 (iota[:, :], iota_c),
                 (dest[:, :, :], dest_c),
                 (strict[:, :], strict_c),
                 (below[:, :, :], below_c),
                 (padrow[:, D:ROW].bitcast(I32), padmeta_c),
                 (maskrow[:, :], mask_v),
                 (maskbc[:, :], mask_v.broadcast_to([128, BATCH * T])))
        ALL_CONST = 16 * len(small)

        def flat(ap):
            return ap.rearrange("p a b -> p (a b)")

        def heads(ap):
            return ap.rearrange("p (h s) -> p h s", h=HALF)

        def seqs(ap):
            return ap.rearrange("p (b s) -> p b s", b=GROUP)

        block = stack.enter_context(nc.Block())

        @block.sync
        def _(sp):
            sp.dma_start(xs[:, 0:GROUP, :], x_v[:, 0:GROUP, :]).then_inc(s_x, 16)
            for dst, src in small:
                sp.dma_start(dst, src).then_inc(s_const, 16)
            for b in range(GROUP):
                sp.dma_start(ctxs[:, b, :, :], ctxT[:, b, :, :]).then_inc(s_ctx[b], 16)
            sp.dma_start(w1s[:, :, :], w1.rearrange("e d h -> d e h")).then_inc(s_ffnw, 16)
            sp.wait_ge(s_setup, 4)
            for i in range(SPARE):
                at = EXPERTS * REGION + 128 * i
                sp.dma_start(rows[at:at + 128, :], padrow[:, :]).then_inc(s_pads, 16)
            with sp.Fori(1, GROUPS) as g:
                sp.wait_ge(s_x, 16 * g)
                sp.dma_start(xs[:, bass.ds(GROUP * g, GROUP), :],
                             x_v[:, bass.ds(GROUP * g, GROUP), :]).then_inc(s_x, 16)
                for b in range(GROUP):
                    sp.wait_ge(s_proj, GROUP * g + (b - GROUP + 1))
                    sp.dma_start(ctxs[:, b, :, :],
                                 ctxT[:, bass.ds(GROUP * g + b, 1), :, :]
                                 .rearrange("p o c t -> p (o c) t")).then_inc(s_ctx[b], 16)
            for e in range(EXPERTS):
                sp.dma_start(w2s[:, e, :, :], w2[e, :, :].rearrange("(c p) d -> p c d", p=128)
                             ).then_inc(s_ffnw, 16)
            sp.wait_ge(s_plan, PLAN)
            sp.wait_ge(s_pads, 16 * SPARE)
            for e in range(EXPERTS):
                r = sp.value_load(pad_row[0:1, e:e + 1], min_val=0, max_val=EXPERTS * REGION - 128)
                sp.dma_start(rows[bass.ds(r, 128), :], padrow[:, :]).then_inc(s_pads, 16)
            sp.wait_ge(s_pads, 16 * (SPARE + EXPERTS))
            sp.wait_ge(s_send, SEND * GROUPS)

            def load(j, r, first):
                at = sp.value_load(slot_row[0:1, j:j + 1] if isinstance(j, int)
                                   else slot_row[0:1, bass.ds(j, 1)],
                                   min_val=0, max_val=(EXPERTS + 1) * REGION - 128)
                if not first:
                    sp.wait_ge(f_send[r], 2 * (j - r))
                sp.dma_start(xg[:, r, :], rows[bass.ds(at, 128), :]).then_inc(f_load[r], 16)

            for r in range(RING):
                load(r, r, True)
            with sp.Fori(1, SLOTS // RING) as q:
                for r in range(RING):
                    load(RING * q + r, r, False)
            for r in range(RING):
                sp.wait_ge(f_send[r], 16 * (SLOTS // RING))
            for j in range(2):
                sp.dma_start(yb[:, j, :, :, :], picked_v[:, GROUP * j:GROUP * (j + 1), :, :]
                             ).then_inc(s_yb[j], 16)
            with sp.Fori(1, GROUPS // 2) as q:
                for j in range(2):
                    G = 2 * q + j
                    sp.wait_ge(s_y2, G - 1)
                    sp.dma_start(yb[:, j, :, :, :], picked_v[:, bass.ds(GROUP * G, GROUP), :, :]
                                 ).then_inc(s_yb[j], 16)
            sp.wait_ge(s_out, 16 * GROUPS)

        @block.gpsimd
        def _(pool):
            nc.gpsimd.memset(minus_half[:, :], -0.5).then_inc(s_zero, 1)
            nc.gpsimd.memset(onesrow[:, :], 0.0).then_inc(s_zero, 1)
            nc.gpsimd.memset(vals[:, :, :, :], 0.0).then_inc(s_zero, 1)
            nc.gpsimd.memset(penalty[:, :], 0.0).then_inc(s_zero, 1)
            pool.wait_ge(s_zero, 4)
            nc.gpsimd.memset(onesrow[0:1, :], 1.0).then_inc(s_pool0, 1)
            nc.gpsimd.memset(vals[:, :, :, HD:HD + 1], 1.0).then_inc(s_pool0, 1)

            def step(g, k):
                G = group(g, 0)
                if k == 1 and G is not None:
                    pool.wait_ge(s_ln1, G + 1)
                    wait(pool, s_xn, GROUP * G)
                    nc.gpsimd.tensor_tensor(rs1[:, :], ve1[:, :], minus_half[:, :],
                                            ALU.pow).then_inc(s_rs1, 1)
                G = group(g, LAG_OUT)
                if k == 2 and G is not None:
                    pool.wait_ge(s_ln2, G + 1)
                    wait(pool, s_x2n, GROUP * G)
                    nc.gpsimd.tensor_tensor(rs2[:, :], ve2[:, :], minus_half[:, :],
                                            ALU.pow).then_inc(s_rs2, 1)
                G = group(g, LAG_SEND)
                if k in (0, 1) and G is not None:
                    pool.wait_ge(s_pos, POS * G + 4)
                    pool.wait_ge(s_rt, ROUTE * G + ROUTE)
                    pool.wait_ge(s_xr, 2 * G + 2)
                    settled()
                    for b in range(GROUP):
                        nc.gpsimd.indirect_dma_start(
                            out=rows, out_offset=bass.IndirectOffsetOnAxis(ap=posi[:, k, b:b + 1], axis=0),
                            in_=xr[:, k, b, :], in_offset=None).then_inc(s_send, 16)
                n = sequence(g, k, LAG_PROJ)
                if n is not None:
                    r = (k - LAG_PROJ) % 2
                    pool.wait_ge(s_k, n + 1)
                    wait(pool, s_sc, 2 * (n - 1))
                    nc.gpsimd.tensor_tensor(
                        kblk[:, r, :, :], kT[:, r, :].unsqueeze(1).broadcast_to([128, HEADS, T]),
                        headmask[:, :].unsqueeze(2).broadcast_to([128, HEADS, T]),
                        ALU.mult).then_inc(s_kb, 1)
                G = group(g, 0)
                if k == 3 and G is not None:
                    pool.wait_ge(s_xn, GROUP * G + GROUP)
                    nc.gpsimd.tensor_tensor(
                        xs[:, bass.ds(GROUP * G, GROUP), :], xs[:, bass.ds(GROUP * G, GROUP), :],
                        bout_g[:, :].unsqueeze(1).broadcast_to([128, GROUP, D]),
                        ALU.add).then_inc(s_xb, 1)

            pool.wait_ge(s_setup, 4)
            bound = pool.to_reg(PICKS - 1)
            carriers = []

            def settled():
                carriers.append(None)
                c = len(carriers) % 32
                return nc.gpsimd.tensor_tensor(pscratch[0:1, c:c + 1], minus_half[0:1, 0:1],
                                               minus_half[0:1, 0:1], ALU.add)

            each_step(pool, step)

            def send(j, r):
                pool.wait_ge(f_y, j + 1)
                wait(pool, f_settled, j)
                settled().then_inc(f_settled, 1)
                nc.gpsimd.indirect_dma_start(
                    out=picked, out_offset=bass.IndirectOffsetOnAxis(
                        ap=xg[:, r, D + 1:D + 2].bitcast(I32), axis=0),
                    in_=yo[:, r, :], in_offset=None, bounds_check=bound,
                    oob_is_err=False).then_inc(f_send[r], 16)

            for r in range(RING):
                send(r, r)
            with pool.Fori(1, SLOTS // RING) as q:
                for r in range(RING):
                    send(RING * q + r, r)

        @block.scalar
        def _(act):
            act.wait_ge(s_const, ALL_CONST)
            nc.scalar.activation(tgates[:, :], gates[:, :], ACT.Tanh).then_inc(s_gate, 1)

            def step(g, k):
                G = group(g, LAG_ROUTE)
                if k == 2 and G is not None:
                    wait(act, s_send, SEND * G)
                    for i in range(2):
                        nc.scalar.activation(xr[:, i, :, 0:D], x2n[:, :, :], ACT.Copy).then_inc(s_xr, 1)
                n = sequence(g, k, LAG_PROJ)
                if n is not None:
                    act.wait_ge(s_xT, n + 1)
                    wait(act, s_proj, n - 1)
                    nc.scalar.activation(xnT[:, (k - LAG_PROJ) % 2, :], ps_xT[:, 0:T],
                                         ACT.Copy).then_inc(s_xnT, 1)
                G = group(g, LAG_OUT)
                if k == 0 and G is not None:
                    act.wait_ge(s_onTp, G + 1)
                    wait(act, s_oproj, G)
                    nc.scalar.activation(flat(onT[:, :, :]), ps_tail[:, :], ACT.Copy).then_inc(s_onT, 1)
                if k == 3 and G is not None:
                    act.wait_ge(s_x2Tp, G + 1)
                    wait(act, s_lg, G)
                    nc.scalar.activation(flat(x2nT[:, :, :]), ps_tail[:, :],
                                         ACT.Copy).then_inc(s_x2nT, 1)
                n = sequence(g, k, LAG_PV)
                if n is not None:
                    r = (k - LAG_PV) % 2
                    wait(act, s_pv, n - 1)
                    for h in range(2):
                        act.wait_ge(s_pT, 2 * n + (h + 1))
                        nc.scalar.activation(flat(probT[:, r, HALF * h:HALF * (h + 1), :]),
                                             ps_pT[h][:, :], ACT.Copy).then_inc(s_pTs, 1)
                n = sequence(g, k, LAG_SCORE)
                if n is not None:
                    r = (k - LAG_SCORE) % 2
                    for h in range(2):
                        act.wait_ge(s_cen, 2 * n + (h + 1))
                        p = flat(prob[:, r, HALF * h:HALF * (h + 1), :])
                        nc.scalar.activation(p, p, ACT.Exp, scale=SCALE).then_inc(s_exp, 1)
                G = group(g, LAG_ROUTE)
                if k == 2 and G is not None:
                    act.wait_ge(s_rt, ROUTE * G + 2)
                    nc.scalar.activation(flat(lexp[:, :, :]), flat(lcen[:, :, :]),
                                         ACT.Exp).then_inc(s_lexp, 1)
                if isinstance(g, int) and GROUP * g + k in W1_STEPS:
                    e = GROUP * g + k - W1_STEPS[0]
                    act.wait_ge(s_ffnw, 16)
                    nc.scalar.activation(w1h[:, e, :], w1s[:, e, :], ACT.Copy).then_inc(s_w1h, 1)
                n = sequence(g, k, LAG_PV)
                if n is not None:
                    act.wait_ge(s_pv, n + 1)
                    wait(act, s_o, n)
                    nc.scalar.activation(flat(oT[:, :, :]), ps_o[:, 0:2 * T], ACT.Copy).then_inc(s_oT, 1)

            each_step(act, step)

            def work(q, r):
                j = slot_of(q, r, 0)
                if j is not None:
                    act.wait_ge(f_xT, j + 1)
                    wait(act, f_up, j - 1)
                    nc.scalar.activation(xh[:, r % 2, :], ps_xT[:, 0:128], ACT.Copy).then_inc(f_xh, 1)
                j = slot_of(q, r, 1)
                if j is not None:
                    i = (r - 1) % 2
                    act.wait_ge(f_up, j + 1)
                    wait(act, f_hT, j - 1)
                    nc.scalar.activation(hid[:, i, :, :], heads(ps_score[i][:, :]),
                                         ACT.Gelu).then_inc(f_gelu, 1)

            each_slot(act, work)
            for G in range(GROUPS):
                act.wait_ge(s_y2, G + 1)
                act.dma_start(out_v[:, GROUP * G:GROUP * (G + 1), :],
                              xs[:, GROUP * G:GROUP * (G + 1), :]).then_inc(s_out, 16)

        @block.vector
        def _(dve):
            dve.wait_ge(s_const, ALL_CONST)
            dve.wait_ge(s_zero, 4)
            nc.vector.tensor_scalar(penalty[0:1, :], maskrow[:, :], -1.0, MASKED,
                                    ALU.add, ALU.mult).then_inc(s_setup, 1)
            dve.wait_ge(s_gate, 1)
            nc.vector.tensor_scalar(flat(wout_g[:, :, :]), flat(wout[:, :, :]), tgates[:, 0:1], None,
                                    ALU.mult).then_inc(s_setup, 1)
            nc.vector.tensor_scalar(bout_g[:, :], bout[:, :], tgates[:, 0:1], None,
                                    ALU.mult).then_inc(s_setup, 1)
            nc.vector.memset(before[:, :], 0.0)
            nc.vector.memset(ones_b[:, :], 1.0)
            nc.vector.memset(padrow[:, 0:D], 0.0)
            nc.vector.tensor_copy(strict_b[:, :], strict[:, :])
            nc.vector.tensor_scalar(regions[:, :], iota8, float(REGION), None, ALU.mult)
            dve.wait_ge(s_setup, 3)
            nc.vector.memset(rsum[:, :, :], 1.0).then_inc(s_setup, 1)
            dve.wait_ge(s_setup, 4)

            carriers = []

            def settled():
                carriers.append(None)
                c = len(carriers) % 32
                nc.vector.memset(scratch[:, c:c + 1], 0.0)

            def statistics(G, s, st, mv, ve, nm, done, used):
                wait(dve, used, GROUP * G)
                settled()
                for b in range(GROUP):
                    nc.vector.bn_stats(st[:, b, :], xs[:, bass.ds(GROUP * G + b, 1), :]
                                       .rearrange("p o d -> p (o d)")).then_inc(s, 1)
                dve.wait_ge(s, STATS * G + GROUP)
                settled()
                for b in range(GROUP):
                    nc.vector.bn_aggr(mv[:, b, :], st[:, b, :]).then_inc(s, 1)
                dve.wait_ge(s, STATS * G + STATS)
                nc.vector.tensor_scalar(nm[:, :], mv[:, :, 0], -1.0, None, ALU.mult).then_inc(done[0], 1)
                nc.vector.tensor_scalar(ve[:, :], mv[:, :, 1], EPS, None, ALU.add).then_inc(done[1], 1)

            def normalise(G, seqs_of, dst, nm, rs, done):
                for b in seqs_of:
                    nc.vector.tensor_scalar(
                        dst[:, b, :], xs[:, bass.ds(GROUP * G + b, 1), :].rearrange("p o d -> p (o d)"),
                        nm[:, b:b + 1], rs[:, b:b + 1], ALU.add, ALU.mult).then_inc(done, 1)

            def route(G):
                at = [0]

                def then(ins):
                    at[0] += 1
                    ins.then_inc(s_rt, 1)

                def done(back=0):
                    dve.wait_ge(s_rt, ROUTE * G + (at[0] - back))

                logits = seqs(ps_tail[:, :])[:, :, 0:EXPERTS]

                def per_expert(ap):
                    return ap.unsqueeze(2).broadcast_to([128, GROUP, EXPERTS])

                dve.wait_ge(s_lg, G + 1)
                then(nc.vector.tensor_reduce(lmax[:, :], logits, AX.X, ALU.max))
                done()
                then(nc.vector.tensor_tensor(lcen[:, :, :], logits, per_expert(lmax[:, :]),
                                             ALU.subtract))
                dve.wait_ge(s_lexp, G + 1)
                then(nc.vector.tensor_reduce(lsum[:, :], lexp[:, :, :], AX.X, ALU.add))
                done()
                then(nc.vector.reciprocal(linv[:, :], lsum[:, :]))
                done()
                then(nc.vector.tensor_tensor(rprob[:, :, :], lexp[:, :, :], per_expert(linv[:, :]),
                                             ALU.mult))
                done()
                settled()
                for b in range(GROUP):
                    then(nc.vector.max(top[:, b, :], rprob[:, b, :]))
                done()
                settled()
                for b in range(GROUP):
                    then(nc.vector.max_index(topi[:, b, :], top[:, b, :], rprob[:, b, :]))
                done()
                then(nc.vector.tensor_copy(topf[:, :, :], topi[:, :, :]))
                then(nc.vector.scalar_tensor_tensor(tsum[:, :], top[:, :, 0], 1e-9, top[:, :, 1],
                                                    ALU.add, ALU.add))
                done()
                experts = iota8.unsqueeze(1).broadcast_to([128, GROUP, EXPERTS])
                wait(dve, s_pos, POS * G)
                for i in range(2):
                    then(nc.vector.tensor_tensor(sel[:, i, :, :], experts, per_expert(topf[:, :, i]),
                                                 ALU.is_equal))
                then(nc.vector.reciprocal(tinv[:, :], tsum[:, :]))
                done()
                then(nc.vector.tensor_tensor(sel_b[:, :, :], sel[:, 0, :, :], sel[:, 1, :, :], ALU.add))
                then(nc.vector.tensor_scalar(tw[:, :], tinv[:, :], tgates[:, 1:2], None, ALU.mult))
                done()
                then(nc.vector.tensor_reduce(picks[:, :], sel_b[:, :, :].rearrange("p b e -> p e b"),
                                             AX.X, ALU.add))
                wait(dve, s_send, SEND * G)
                then(nc.vector.tensor_tensor(
                    xr[:, :, :, D].rearrange("p k b -> p b k"), top[:, :, 0:2],
                    tw[:, :].unsqueeze(2).broadcast_to([128, GROUP, 2]), ALU.mult))
                then(nc.vector.tensor_copy(
                    xr[:, :, :, D + 1].bitcast(I32),
                    dest[:, bass.ds(GROUP * G, GROUP), :].rearrange("p b k -> p k b")))
                done()
                assert at[0] == ROUTE

            def position(G):
                dve.wait_ge(s_rank, G + 1)
                wait(dve, s_send, SEND * G)
                nc.vector.tensor_tensor(
                    place[:, :, :], ps_tail[:, 0:GROUP * EXPERTS].rearrange("p (b e) -> p b e", b=GROUP),
                    regions[:, :].unsqueeze(1).broadcast_to([128, GROUP, EXPERTS]),
                    ALU.add).then_inc(s_pos, 1)
                dve.wait_ge(s_pos, POS * G + 1)
                nc.vector.tensor_tensor(
                    placed[:, :, :, :], sel[:, :, :, :],
                    place[:, :, :].unsqueeze(1).broadcast_to([128, 2, GROUP, EXPERTS]),
                    ALU.mult).then_inc(s_pos, 1)
                dve.wait_ge(s_pos, POS * G + 2)
                nc.vector.tensor_reduce(pos[:, :, :], placed[:, :, :, :], AX.X, ALU.add).then_inc(s_pos, 1)
                dve.wait_ge(s_pos, POS * G + 3)
                nc.vector.tensor_copy(posi[:, :, :], pos[:, :, :]).then_inc(s_pos, 1)
                nc.vector.tensor_tensor(before[:, :], before[:, :], picks[:, :], ALU.add).then_inc(s_pos, 1)
                dve.wait_ge(s_pos, POS * G + POS)

            def plan():
                at = [0]

                def then(ins):
                    at[0] += 1
                    ins.then_inc(s_plan, 1)
                    dve.wait_ge(s_plan, at[0])

                dve.wait_ge(s_total, 1)
                then(nc.vector.tensor_copy(total[:, :], ps_tail[:, 0:EXPERTS]))
                then(nc.vector.tensor_tensor(prow[:, :], total[:, :], regions[:, :], ALU.add))
                then(nc.vector.tensor_copy(pad_row[:, :], prow[:, :]))
                then(nc.vector.tensor_scalar(srow[:, 0:BATCH], iota[:, 0:BATCH], 128.0, None, ALU.mult))
                then(nc.vector.tensor_tensor(
                    more[:, :, :], total[:, :].unsqueeze(2).broadcast_to([128, EXPERTS, BATCH]),
                    srow[:, 0:BATCH].unsqueeze(1).broadcast_to([128, EXPERTS, BATCH]), ALU.is_gt))
                then(nc.vector.tensor_reduce(nslots[:, :], more[:, :, :], AX.X, ALU.add))
                then(nc.vector.tensor_tensor(
                    upto[:, :, :], below[:, :, :],
                    nslots[:, :].unsqueeze(1).broadcast_to([128, EXPERTS, EXPERTS]), ALU.mult))
                then(nc.vector.tensor_reduce(ends[:, :], upto[:, :, :], AX.X, ALU.add))
                then(nc.vector.tensor_tensor(
                    past[:, :, :], iota[:, 0:SLOTS].unsqueeze(2).broadcast_to([128, SLOTS, EXPERTS]),
                    ends[:, :].unsqueeze(1).broadcast_to([128, SLOTS, EXPERTS]), ALU.is_ge))
                then(nc.vector.tensor_tensor(
                    gone[:, :, :], past[:, :, :],
                    nslots[:, :].unsqueeze(1).broadcast_to([128, SLOTS, EXPERTS]), ALU.mult))
                then(nc.vector.tensor_reduce(sexp[:, :], past[:, :, :], AX.X, ALU.add))
                then(nc.vector.tensor_reduce(sgone[:, :], gone[:, :, :], AX.X, ALU.add))
                then(nc.vector.tensor_tensor(srow[:, :], iota[:, 0:SLOTS], sgone[:, :], ALU.subtract))
                then(nc.vector.tensor_scalar(sgone[:, :], srow[:, :], 128.0, None, ALU.mult))
                then(nc.vector.scalar_tensor_tensor(slot_row[:, :], sexp[:, :], float(REGION),
                                                    sgone[:, :], ALU.mult, ALU.add))
                then(nc.vector.tensor_scalar(slot_exp[:, :], sexp[:, :], float(EXPERTS - 1), None,
                                             ALU.min))
                assert at[0] == PLAN

            def step(g, k):
                G = group(g, LAG_SEND)
                if k == 0 and G is not None:
                    position(G)
                G = group(g, LAG_OUT)
                if k == 2 and G is not None:
                    dve.wait_ge(s_rs2, G + 1)
                    dve.wait_ge(s_nm2, G + 1)
                    wait(dve, s_x2Tp, G)
                    wait(dve, s_xr, 2 * G)
                    normalise(G, range(GROUP), x2n, nm2, rs2, s_x2n)
                G = group(g, 0)
                if k == 2 and G is not None:
                    dve.wait_ge(s_rs1, G + 1)
                    dve.wait_ge(s_nm1, G + 1)
                    wait(dve, s_xT, GROUP * (G - 1) + 2)
                    normalise(G, range(2), xn, nm1, rs1, s_xn)
                n = sequence(g, k, LAG_SCORE)
                if n is not None:
                    r = (k - LAG_SCORE) % 2
                    wait(dve, s_cen, 2 * (n - 1))
                    for h in range(2):
                        dve.wait_ge(s_sc, 2 * n + (h + 1))
                        nc.vector.tensor_reduce(rowmax[:, r, HALF * h:HALF * (h + 1)],
                                                heads(ps_score[h][:, :]), AX.X, ALU.max
                                                ).then_inc(s_max, 1)
                    wait(dve, s_pT, 2 * (n - 1))
                    for h in range(2):
                        dve.wait_ge(s_max, 2 * n + (h + 1))
                        nc.vector.tensor_tensor(
                            prob[:, r, HALF * h:HALF * (h + 1), :], heads(ps_score[h][:, :]),
                            rowmax[:, r, HALF * h:HALF * (h + 1)].unsqueeze(2)
                            .broadcast_to([128, HALF, T]), ALU.subtract).then_inc(s_cen, 1)
                n = sequence(g, k, LAG_O)
                if n is not None:
                    r = (k - LAG_O) % 2
                    o3 = ps_o[:, 0:2 * T].rearrange("p (h c) -> p h c", c=VPAD)
                    dve.wait_ge(s_o, n + 1)
                    wait(dve, s_on, n - 1)
                    nc.vector.reciprocal(rsum[:, r, :], o3[:, :, HD]).then_inc(s_rsum, 1)
                    dve.wait_ge(s_rsum, n + 1)
                    wait(dve, s_onTp, g - LAG_O // GROUP)
                    nc.vector.tensor_tensor(
                        on[:, (k - LAG_O) % GROUP, :].rearrange("p (h c) -> p h c", c=HD),
                        o3[:, :, 0:HD], rsum[:, r, :].unsqueeze(2).broadcast_to([128, HEADS, HD]),
                        ALU.mult).then_inc(s_on, 1)
                n = sequence(g, k, LAG_PROJ)
                if n is not None:
                    r = (k - LAG_PROJ) % 2
                    cols = bass.ds(n * T, T)
                    dve.wait_ge(s_proj, n + 1)
                    wait(dve, s_kb, n - 1)
                    nc.vector.scalar_tensor_tensor(kT[:, r, :], ps_proj[:, 0:T], bkey[:, :],
                                                   maskbc[:, cols], ALU.add, ALU.mult).then_inc(s_k, 1)
                    wait(dve, s_sc, 2 * (n - 1))
                    nc.vector.scalar_tensor_tensor(qT[:, r, :], ps_proj[:, T:2 * T], bqry[:, :],
                                                   maskbc[:, cols], ALU.add, ALU.mult).then_inc(s_q, 1)
                    wait(dve, s_pv, n - 3)
                    nc.vector.tensor_tensor(
                        vals[:, (k - LAG_PROJ) % 4, :, 0:HD],
                        ps_proj[:, 2 * T:3 * T].rearrange("p (h c) -> p h c", c=HD),
                        bval[:, :].rearrange("p (h c) -> p h c", c=HD), ALU.add).then_inc(s_v, 1)
                    dve.wait_ge(s_xb, g)
                    x1 = xs[:, bass.ds(n, 1), :].rearrange("p o d -> p (o d)")
                    nc.vector.tensor_tensor(x1, ps_proj[:, 3 * T:4 * T], x1, ALU.add).then_inc(s_xo, 1)
                G = group(g, 0)
                if k == 0 and G is not None:
                    dve.wait_ge(s_x, 16 * (G + 1))
                    statistics(G, s_st1, st1, mv1, ve1, nm1, (s_nm1, s_ln1), s_xn)
                G = group(g, LAG_OUT)
                if k == 1 and G is not None:
                    dve.wait_ge(s_oproj, G + 1)
                    wait(dve, s_xo, GROUP * G + GROUP)
                    x4 = xs[:, bass.ds(GROUP * G, GROUP), :]
                    nc.vector.tensor_tensor(x4, seqs(ps_tail[:, :]), x4, ALU.add).then_inc(s_x2, 1)
                    dve.wait_ge(s_x2, G + 1)
                    statistics(G, s_st2, st2, mv2, ve2, nm2, (s_nm2, s_ln2), s_x2n)
                G = group(g, LAG_ROUTE)
                if k == 2 and G is not None:
                    route(G)
                G = group(g, 0)
                if k == 3 and G is not None:
                    wait(dve, s_xT, GROUP * G)
                    normalise(G, range(2, GROUP), xn, nm1, rs1, s_xn)
                if isinstance(g, int) and GROUP * g + k in W1_STEPS:
                    e = GROUP * g + k - W1_STEPS[0]
                    dve.wait_ge(s_w1h, e + 1)
                    nc.vector.tensor_tensor(w1l[:, e, :], w1s[:, e, :], w1h[:, e, :].bitcast(F32),
                                            ALU.subtract).then_inc(s_w1l, 1)

            each_step(dve, step)
            plan()

            def work(q, r):
                j = slot_of(q, r, 0)
                if j is not None:
                    dve.wait_ge(f_xh, j + 1)
                    wait(dve, f_up, j - 1)
                    nc.vector.tensor_tensor(xl[:, r % 2, :], ps_xT[:, 0:128],
                                            xh[:, r % 2, :].bitcast(F32), ALU.subtract).then_inc(f_xl, 1)
                j = slot_of(q, r, 2)
                if j is not None:
                    i = (r - 2) % 2
                    dve.wait_ge(f_hT, j + 1)
                    wait(dve, f_down, j - 1)
                    nc.vector.tensor_copy(hidT[:, i, :, :], heads(ps_pT[i][:, :])).then_inc(f_hTs, 1)
                j = slot_of(q, r, 3)
                if j is not None:
                    i = (r - 3) % RING
                    dve.wait_ge(f_down, j + 1)
                    wait(dve, f_send[i], 2 * (j - i))
                    nc.vector.tensor_scalar(yo[:, i, :], ps_y[i % 2][:, 0:D], xg[:, i, D:D + 1], None,
                                            ALU.mult).then_inc(f_y, 1)

            each_slot(dve, work)

            def add_picks(q):
                for j in range(2):
                    G = 2 * q + j
                    x4 = xs[:, bass.ds(GROUP * G, GROUP), :]
                    dve.wait_ge(s_yb[j], 16 * (q + 1))
                    nc.vector.tensor_tensor(x4, x4, yb[:, j, :, 0, :], ALU.add).then_inc(s_y1, 1)
                    dve.wait_ge(s_y1, G + 1)
                    nc.vector.tensor_tensor(x4, x4, yb[:, j, :, 1, :], ALU.add).then_inc(s_y2, 1)

            with dve.Fori(0, GROUPS // 2) as q:
                add_picks(q)

        @block.tensor
        def _(pe):
            pe.wait_ge(s_const, ALL_CONST)
            pe.wait_ge(s_pool0, 2)
            pe.wait_ge(s_setup, 4)

            def step(g, k):
                n = sequence(g, k, LAG_PROJ)
                if n is not None:
                    pe.wait_ge(s_xn, n + 1)
                    wait(pe, s_xnT, n)
                    nc.tensor.transpose(ps_xT[:, 0:T], xn[:, (k - LAG_PROJ) % GROUP, :],
                                        ident[:, :]).then_inc(s_xT, 1)
                G = group(g, LAG_OUT)
                if k == 1 and G is not None:
                    pe.wait_ge(s_onT, G + 1)
                    for b in range(GROUP):
                        last = nc.tensor.matmul(ps_tail[:, b * D:(b + 1) * D], onT[:, b, :],
                                                wout_g[:, 1, :], start=True, stop=True)
                    last.then_inc(s_oproj, 1)
                if k == 3 and G is not None:
                    pe.wait_ge(s_x2n, GROUP * G + GROUP)
                    wait(pe, s_rt, ROUTE * (G - 1) + 2)
                    for b in range(GROUP):
                        last = nc.tensor.transpose(ps_tail[:, b * T:(b + 1) * T], x2n[:, b, :], ident[:, :])
                    last.then_inc(s_x2Tp, 1)
                G = group(g, LAG_ROUTE)
                if k == 2 and G is not None:
                    pe.wait_ge(s_x2nT, G + 1)
                    wait(pe, s_x2, min(G + 2, GROUPS) if isinstance(G, int) else G + 2)
                    wait(pe, s_pos, POS * (G - 1) + 1)
                    for b in range(GROUP):
                        last = nc.tensor.matmul(ps_tail[:, b * 128:(b + 1) * 128], x2nT[:, b, :],
                                                router[:, :], start=True, stop=True)
                    last.then_inc(s_lg, 1)
                n = sequence(g, k, LAG_SCORE)
                if n is not None:
                    r = (k - LAG_SCORE) % 2
                    pe.wait_ge(s_q, n + 1)
                    pe.wait_ge(s_kb, n + 1)
                    for h in range(2):
                        wait(pe, s_cen, 2 * n + (h - 1))
                        nc.tensor.matmul(ps_score[h][:, :], qT[:, r, :],
                                         flat(kblk[:, r, HALF * h:HALF * (h + 1), :]),
                                         start=True, stop=False)
                        nc.tensor.matmul(ps_score[h][:, :], onesrow[:, :],
                                         penalty[:, bass.ds(n * T, T)].unsqueeze(1)
                                         .broadcast_to([128, HALF, T]),
                                         start=False, stop=True).then_inc(s_sc, 1)
                G = group(g, LAG_OUT)
                if k == 0 and G is not None:
                    pe.wait_ge(s_on, GROUP * G + GROUP)
                    wait(pe, s_x2nT, G)
                    wait(pe, s_pos, POS * (G - 2) + 1)
                    for b in range(GROUP):
                        last = nc.tensor.transpose(ps_tail[:, b * T:(b + 1) * T], on[:, b, :], ident[:, :])
                    last.then_inc(s_onTp, 1)
                n = sequence(g, k, LAG_O)
                if n is not None:
                    pe.wait_ge(s_oT, n + 1)
                    for h in range(2):
                        last = nc.tensor.transpose(ps_o[:, h * T:(h + 1) * T], oT[:, h, :], ident[:, :])
                    last.then_inc(s_o, 1)
                n = sequence(g, k, LAG_PV)
                if n is not None:
                    r = (k - LAG_PV) % 2
                    for h in range(2):
                        pe.wait_ge(s_exp, 2 * n + (h + 1))
                        wait(pe, s_pTs, 2 * n + (h - 1))
                        for j in range(HALF):
                            last = nc.tensor.transpose(ps_pT[h][:, j * T:(j + 1) * T],
                                                       prob[:, r, HALF * h + j, :], ident[:, :])
                        last.then_inc(s_pT, 1)
                n = sequence(g, k, LAG_PROJ)
                if n is not None:
                    r = (k - LAG_PROJ) % 2
                    b = (k - LAG_PROJ) % GROUP
                    pe.wait_ge(s_xnT, n + 1)
                    pe.wait_ge(s_ctx[b], 16 * g)
                    wait(pe, s_xo, n)
                    for c in range(FCH):
                        nc.tensor.matmul(ps_proj[:, 0:T], wsrc[:, c, 0:D], ctxs[:, b, c, :],
                                         start=(c == 0), stop=(c == FCH - 1))
                    nc.tensor.matmul(ps_proj[:, T:2 * T], wtgt[:, :], xnT[:, r, :], start=True, stop=True)
                    for c in range(FCH):
                        nc.tensor.matmul(ps_proj[:, 2 * T:3 * T], ctxs[:, b, c, :], wsrc[:, c, D:2 * D],
                                         start=(c == 0), stop=(c == FCH - 1))
                    nc.tensor.matmul(ps_proj[:, 3 * T:4 * T], xnT[:, r, :], wout_g[:, 0, :],
                                     start=True, stop=True).then_inc(s_proj, 1)
                n = sequence(g, k, LAG_PV)
                if n is not None:
                    r = (k - LAG_PV) % 2
                    pe.wait_ge(s_pTs, 2 * n + 2)
                    pe.wait_ge(s_v, n + 1)
                    wait(pe, s_on, n)
                    for h in range(HEADS):
                        q = h % HALF
                        last = nc.tensor.matmul(
                            ps_o[VPAD * q:VPAD * (q + 1), (h // HALF) * T:(h // HALF + 1) * T],
                            vals[:, (k - LAG_PV) % 4, h, :], probT[:, r, h, :], start=True, stop=True)
                    last.then_inc(s_pv, 1)

                G = group(g, LAG_ROUTE)
                if k == 3 and G is not None:
                    pe.wait_ge(s_rt, ROUTE * G + 21)
                    pe.wait_ge(s_x2nT, min(G + 2, GROUPS) if isinstance(G, int) else G + 2)
                    nc.tensor.matmul(ps_tail[:, 0:GROUP * EXPERTS], strict_b[:, :], flat(sel_b[:, :, :]),
                                     start=True, stop=False)
                    for b in range(GROUP - 1):
                        left = GROUP - 1 - b
                        nc.tensor.matmul(
                            ps_tail[:, EXPERTS * (b + 1):EXPERTS * GROUP], ones_b[:, :],
                            sel_b[:, b, :].unsqueeze(1).broadcast_to([128, left, EXPERTS]),
                            start=False, stop=False)
                    nc.tensor.matmul(ps_tail[:, 0:GROUP * EXPERTS], ones_b[:, :],
                                     before[:, :].unsqueeze(1).broadcast_to([128, GROUP, EXPERTS]),
                                     start=False, stop=True).then_inc(s_rank, 1)

            each_step(pe, step)
            pe.wait_ge(s_pos, POS * GROUPS)
            nc.tensor.matmul(ps_tail[:, 0:EXPERTS], ones_b[:, :], before[:, :], start=True,
                             stop=True).then_inc(s_total, 1)

            pe.wait_ge(s_ffnw, 16 * (1 + EXPERTS))
            pe.wait_ge(s_w1l, EXPERTS)
            pe.wait_ge(s_plan, PLAN)

            def expert(j):
                at = slot_exp[0:1, j:j + 1] if isinstance(j, int) else slot_exp[0:1, bass.ds(j, 1)]
                return bass.ds(pe.value_load(at, min_val=0, max_val=EXPERTS - 1), 1)

            def work(q, r):
                j = slot_of(q, r, 0)
                if j is not None:
                    pe.wait_ge(f_load[r], 2 * (j - r) + 16)
                    wait(pe, f_xl, j)
                    nc.tensor.transpose(ps_xT[:, 0:128], xg[:, r, 0:D], ident[:, :]).then_inc(f_xT, 1)
                j = slot_of(q, r, 1)
                if j is not None:
                    i = (r - 1) % 2
                    e = expert(j)
                    pe.wait_ge(f_xl, j + 1)
                    wait(pe, f_gelu, j - 1)
                    for a, w, first in ((xh, w1h, True), (xl, w1h, False), (xh, w1l, False)):
                        last = nc.tensor.matmul(ps_score[i][:, :], a[:, i, :],
                                                w[:, e, :].rearrange("p o h -> p (o h)"),
                                                start=first, stop=(w is w1l))
                    last.then_inc(f_up, 1)
                j = slot_of(q, r, 2)
                if j is not None:
                    i = (r - 2) % 2
                    pe.wait_ge(f_gelu, j + 1)
                    wait(pe, f_hTs, j - 1)
                    for c in range(HCH):
                        last = nc.tensor.transpose(ps_pT[i][:, c * 128:(c + 1) * 128], hid[:, i, c, :],
                                                   ident[:, :])
                    last.then_inc(f_hT, 1)
                j = slot_of(q, r, 3)
                if j is not None:
                    i = (r - 3) % 2
                    e = expert(j)
                    pe.wait_ge(f_hTs, j + 1)
                    wait(pe, f_y, j - 1)
                    for c in range(HCH):
                        last = nc.tensor.matmul(ps_y[i][:, 0:D], hidT[:, i, c, :],
                                                w2s[:, e, c, :].rearrange("p o d -> p (o d)"),
                                                start=(c == 0), stop=(c == HCH - 1))
                    last.then_inc(f_down, 1)

            each_slot(pe, work)


def kernel(x, ctx_2048, mask_BxS2_fk1, g_xattn, g_ffn, L0_xattn_W_src, L0_xattn_b_src,
           L0_xattn_W_tgt, L0_xattn_b_tgt, L0_xattn_W_out, L0_xattn_b_out, L0_ffn_router_w,
           L0_ffn_w1, L0_ffn_w2):
    import numpy as np
    import concourse.bacc as bacc
    from concourse.bass_utils import run_bass_kernel_spmd

    router = np.zeros((128, 128), np.float32)
    router[:, :EXPERTS] = np.asarray(L0_ffn_router_w).T
    ctx = np.asarray(ctx_2048)
    arrays = {
        "x": x, "ctxT": ctx.transpose(2, 0, 1).reshape(FCH, 128, BATCH, T).transpose(1, 2, 0, 3),
        "mask": mask_BxS2_fk1, "g_xattn": g_xattn, "g_ffn": g_ffn,
        "w_srcT": np.asarray(L0_xattn_W_src).T, "b_src": L0_xattn_b_src,
        "w_tgtT": np.asarray(L0_xattn_W_tgt).T, "b_tgt": L0_xattn_b_tgt,
        "w_outT": np.asarray(L0_xattn_W_out).T, "b_out": L0_xattn_b_out,
        "routerT": router, "w1": L0_ffn_w1, "w2": L0_ffn_w2,
        "ident_c": np.eye(128, dtype=np.float32),
        "headmask_c": np.kron(np.eye(HEADS), np.ones((HD, 1))).astype(np.float32),
        "iota_c": np.tile(np.arange(SLOTS + EXPERTS, dtype=np.float32), (128, 1)),
        "dest_c": (np.arange(PICKS, dtype=np.int32).reshape(BATCH, T, 2)).transpose(1, 0, 2),
        "strict_c": np.triu(np.ones((128, 128), np.float32), 1),
        "below_c": np.tile(np.tril(np.ones((EXPERTS, EXPERTS), np.float32)), (128, 1, 1)),
        "padmeta_c": np.tile(np.array([0, NOWHERE], np.int32), (128, 1)),
    }
    nc = bacc.Bacc("TRN2", target_bir_lowering=False, num_devices=1)
    arrays = {k: np.ascontiguousarray(a) for k, a in arrays.items()}
    args = {k: nc.dram_tensor(k, a.shape, mybir.dt.from_np(a.dtype), kind="ExternalInput").ap()
            for k, a in arrays.items()}
    out = nc.dram_tensor("out", [BATCH, T, D], F32, kind="ExternalOutput").ap()
    rows = nc.dram_tensor("rows", [(EXPERTS + 1) * REGION, ROW], F32, kind="Internal").ap()
    picked = nc.dram_tensor("picked", [PICKS, D], F32, kind="Internal").ap()
    gated_cross_attention_moe(nc, out=out, rows=rows, picked=picked, **args)
    r = run_bass_kernel_spmd(nc, [arrays], core_ids=[0])
    return r.results[0]["out"]
```

```python
from contextlib import ExitStack

import concourse.bass as bass
from concourse import mybir

F32 = mybir.dt.float32
BF16 = mybir.dt.bfloat16
U32 = mybir.dt.uint32
I32 = mybir.dt.int32
F32R = mybir.dt.float32r
ALU = mybir.AluOpType
ACT = mybir.ActivationFunctionType
AX = mybir.AxisListType

BATCH = 32
T = 128
D = 128
SRC = 256
FCH = SRC // 128
HEADS = 8
HD = D // HEADS
HALF = HEADS // 2
VPAD = 32
EXPERTS = 8
HID = 512
HCH = HID // 128
GROUP = 4
GROUPS = BATCH // GROUP
EPS = 1e-5
SCALE = float(HD) ** -0.5
MASKED = 1e30

LAG_PROJ = 4
LAG_SCORE = 6
LAG_PV = 7
LAG_O = 8
LAG_OUT = 3
LAG_ROUTE = 4
LAG_SEND = 5
STEADY = LAG_SEND
DRAINED = GROUPS + LAG_SEND

ROW = D + 2
CAP = BATCH * T
REGION = CAP + 128
PICKS = 2 * BATCH * T
RING = 8
XRING = 4
LAG_UP = 2
LAG_HT = 3
LAG_DOWN = 4
SLOTS = PICKS // 128 + EXPERTS - 1
SPARE = SLOTS - PICKS // 128
NOWHERE = 1 << 20

SENDS = (range(0, 3), range(3, 6), range(6, 8), range(0))
LATE_MAX = (2,)


def each_step(eng, body):
    for g in range(STEADY):
        for k in range(GROUP):
            body(g, k)
    with eng.Fori(STEADY, GROUPS) as g:
        for k in range(GROUP):
            body(g, k)
    for g in range(GROUPS, DRAINED):
        for k in range(GROUP):
            body(g, k)


def sequence(g, k, lag):
    n = GROUP * g + (k - lag)
    if isinstance(n, int) and not 0 <= n < BATCH:
        return None
    return n


def group(g, lag):
    n = g - lag
    if isinstance(n, int) and not 0 <= n < GROUPS:
        return None
    return n


def outbox(G):
    shared = GROUPS - LAG_ROUTE
    if not isinstance(G, int) or G <= shared:
        return 0, G
    i = (G - shared) % 2
    return i, (G - shared - i) // 2 + (shared if i == 0 else 0)


def each_slot(eng, body):
    for r in range(RING):
        body(0, r)
    with eng.Fori(1, SLOTS // RING) as q:
        for r in range(RING):
            body(q, r)
    for n in range(SLOTS // RING * RING, SLOTS + LAG_DOWN):
        body(n // RING, n % RING)


def slot_of(q, r, lag):
    j = RING * q + (r - lag)
    if isinstance(j, int) and not 0 <= j < SLOTS:
        return None
    return j


def wait(eng, sem, value):
    if not isinstance(value, int) or value > 0:
        eng.wait_ge(sem, value)


def gated_cross_attention_moe(nc, x, ctxT, mask, weights, vectors, w1, w2, ident_c, tables_c,
                              integers_c, rows, picked, out):
    with ExitStack() as stack:
        def sb(name, shape, dt=F32):
            return stack.enter_context(nc.sbuf_tensor(name, shape, dt))

        def bank(name, cols=512):
            return stack.enter_context(nc.psum_tensor(name, [128, cols], F32))

        def sem(name):
            return stack.enter_context(nc.semaphore(name))

        ident = sb("ident", [128, 128])
        tables = sb("tables", [128, HEADS + SLOTS + EXPERTS + 128 + EXPERTS * EXPERTS])
        headmask = tables[:, 0:HEADS]
        iota = tables[:, HEADS:HEADS + SLOTS + EXPERTS]
        iota8 = iota[:, 0:EXPERTS]
        strict = tables[:, HEADS + SLOTS + EXPERTS:HEADS + SLOTS + EXPERTS + 128]
        below = tables[:, HEADS + SLOTS + EXPERTS + 128:].rearrange("p (a b) -> p a b", a=EXPERTS)
        integers = sb("integers", [128, PICKS // 128 + 2], I32)
        dest = integers[:, 0:PICKS // 128].rearrange("p (b k) -> p b k", k=2)
        padmeta = integers[:, PICKS // 128:]
        strict_b = sb("strict_b", [128, 128], BF16)
        ones_b = sb("ones_b", [128, 128], BF16)
        padrow = sb("padrow", [128, ROW])
        regions = sb("regions", [128, EXPERTS])
        wts = sb("wts", [128, FCH * SRC + D + 2 * D + 128 + 3])
        wsrc = wts[:, 0:FCH * SRC].rearrange("p (c o) -> p c o", c=FCH)
        wtgt = wts[:, FCH * SRC:FCH * SRC + D]
        wout = wts[:, FCH * SRC + D:FCH * SRC + 3 * D]
        router = wts[:, FCH * SRC + 3 * D:FCH * SRC + 3 * D + 128]
        bkey = wts[:, FCH * SRC + 3 * D + 128:FCH * SRC + 3 * D + 129]
        bqry = wts[:, FCH * SRC + 3 * D + 129:FCH * SRC + 3 * D + 130]
        bval = wts[:, FCH * SRC + 3 * D + 130:]
        vecs = sb("vecs", [128, D + 2])
        bout = vecs[:, 0:D]
        gates = vecs[:, D:]
        wout_g = sb("wout_g", [128, 2, D])
        bout_g = sb("bout_g", [128, D])
        tgates = sb("tgates", [128, 2])
        w1s = sb("w1s", [128, EXPERTS, HID])
        w2s = sb("w2s", [128, EXPERTS, HCH, D])
        maskbc = sb("maskbc", [128, BATCH * T])
        maskrow = sb("maskrow", [1, BATCH * T])
        scratch = sb("scratch", [128, 32])
        pscratch = sb("pscratch", [128, 32])
        ascratch = sb("ascratch", [128, 2])
        minus_half = sb("minus_half", [128, GROUP])
        xs = sb("xs", [128, BATCH, D])
        ctxs = sb("ctxs", [128, GROUP, FCH, T])
        xn = sb("xn", [128, GROUP, D])
        xnT = sb("xnT", [128, 2, T])
        kT = sb("kT", [128, 2, T])
        qT = sb("qT", [128, 2, 2, T])
        kblk = sb("kblk", [128, 2, HEADS, T])
        vals = sb("vals", [128, 4, HEADS, VPAD])
        prob = sb("prob", [128, 2, HEADS, T])
        probT = sb("probT", [128, 2, HEADS, T])
        rowmax = sb("rowmax", [128, 2, HEADS])
        nmax = sb("nmax", [128, 2, HALF])
        oT = sb("oT", [128, 2, T])
        rsum = sb("rsum", [128, 2, HEADS])
        on = sb("on", [128, GROUP, D])
        onT = sb("onT", [128, GROUP, T])
        st1 = sb("st1", [128, GROUP, 6])
        mv1 = sb("mv1", [128, GROUP, 2])
        ve1 = sb("ve1", [128, GROUP])
        nm1 = sb("nm1", [128, GROUP])
        rs1 = sb("rs1", [128, GROUP])
        mr1 = sb("mr1", [128, GROUP])
        st2 = sb("st2", [128, GROUP, 6])
        mv2 = sb("mv2", [128, GROUP, 2])
        ve2 = sb("ve2", [128, GROUP])
        nm2 = sb("nm2", [128, GROUP])
        rs2 = sb("rs2", [128, GROUP])
        x2n = sb("x2n", [128, GROUP, D])
        x2nT = sb("x2nT", [128, GROUP, T])
        lmax = sb("lmax", [128, GROUP])
        lcen = sb("lcen", [128, GROUP, EXPERTS])
        lexp = sb("lexp", [128, GROUP, EXPERTS])
        lsum = sb("lsum", [128, GROUP])
        linv = sb("linv", [128, GROUP])
        topp = sb("topp", [128, GROUP, 2])
        top = sb("top", [128, GROUP, 8])
        topi = sb("topi", [128, GROUP, 8], U32)
        topf = sb("topf", [128, GROUP, 8])
        tsum = sb("tsum", [128, GROUP])
        tinv = sb("tinv", [128, GROUP])
        tw = sb("tw", [128, GROUP])
        sel = sb("sel", [128, 2, GROUP, EXPERTS])
        sel_b = sb("sel_b", [128, GROUP, EXPERTS], BF16)
        before = sb("before", [128, EXPERTS], BF16)
        picks = sb("picks", [128, EXPERTS])
        place = sb("place", [128, GROUP, EXPERTS])
        placed = sb("placed", [128, 2, GROUP, EXPERTS])
        pos = sb("pos", [128, 2, GROUP])
        posi = sb("posi", [128, 2, 2, GROUP], I32)
        xr = sb("xr", [128, 2, 2, GROUP, ROW])
        total = sb("total", [128, EXPERTS])
        more = sb("more", [128, EXPERTS, BATCH])
        nslots = sb("nslots", [128, EXPERTS])
        upto = sb("upto", [128, EXPERTS, EXPERTS])
        ends = sb("ends", [128, EXPERTS])
        past = sb("past", [128, SLOTS, EXPERTS])
        gone = sb("gone", [128, SLOTS, EXPERTS])
        sexp = sb("sexp", [128, SLOTS])
        sgone = sb("sgone", [128, SLOTS])
        srow = sb("srow", [128, SLOTS])
        slot_row = sb("slot_row", [128, SLOTS], I32)
        slot_exp = sb("slot_exp", [128, SLOTS], I32)
        prow = sb("prow", [128, EXPERTS])
        pad_row = sb("pad_row", [128, EXPERTS], I32)
        w1h = sb("w1h", [128, EXPERTS, HID], F32R)
        w1l = sb("w1l", [128, EXPERTS, HID], F32R)
        xg = sb("xg", [128, RING, ROW])
        xh = sb("xh", [128, XRING, 128], F32R)
        xl = sb("xl", [128, XRING, 128], F32R)
        yo = sb("yo", [128, RING, D])
        hid = probT[:, :, 0:HCH, :]
        hidT = probT[:, :, HCH:2 * HCH, :]
        yb = [half.rearrange("p (g b k d) -> p g b k d", b=GROUP, k=2, d=D)[:, g]
              for half in (w1s[:, :, :].rearrange("p e h -> p (e h)"), maskbc[:, :])
              for g in range(GROUPS // 2)]

        ps_score = [bank("ps_score0"), bank("ps_score1")]
        ps_pT = [bank("ps_pT0"), bank("ps_pT1")]
        ps_xT = bank("ps_xT")
        ps_proj = bank("ps_proj")
        ps_o = bank("ps_o")
        ps_tail = bank("ps_tail")
        ps_y = [ps_proj, ps_o]
        ps_x = [ps_xT, ps_tail]

        s_ident = sem("s_ident")
        s_wts = sem("s_wts")
        s_tables = sem("s_tables")
        s_ints = sem("s_ints")
        s_mask0 = sem("s_mask0")
        s_mask = sem("s_mask")
        s_w1 = sem("s_w1")
        s_ffnw = sem("s_ffnw")
        s_x = sem("s_x")
        s_ctx = [sem(f"s_ctx{i}") for i in range(GROUP)]
        s_zero = sem("s_zero")
        s_pool0 = sem("s_pool0")
        s_gate = sem("s_gate")
        s_setup = sem("s_setup")
        s_ones = sem("s_ones")
        s_bias = sem("s_bias")
        s_pad0 = sem("s_pad0")
        s_pen = sem("s_pen")
        s_penal = [sem(f"s_penal{i}") for i in range(2)]
        s_late = sem("s_late")
        s_st1 = sem("s_st1")
        s_nm1 = sem("s_nm1")
        s_ln1 = sem("s_ln1")
        s_rs1 = sem("s_rs1")
        s_mr1 = sem("s_mr1")
        s_xn = sem("s_xn")
        s_xb = sem("s_xb")
        s_xT = sem("s_xT")
        s_xnT = sem("s_xnT")
        s_proj = sem("s_proj")
        s_k = sem("s_k")
        s_q = sem("s_q")
        s_v = sem("s_v")
        s_xo = sem("s_xo")
        s_kb = sem("s_kb")
        s_sc = sem("s_sc")
        s_max = sem("s_max")
        s_cen = sem("s_cen")
        s_exp = sem("s_exp")
        s_pT = sem("s_pT")
        s_pTs = sem("s_pTs")
        s_pv = sem("s_pv")
        s_oT = sem("s_oT")
        s_o = sem("s_o")
        s_rsum = sem("s_rsum")
        s_on = sem("s_on")
        s_onTp = sem("s_onTp")
        s_onT = sem("s_onT")
        s_oproj = sem("s_oproj")
        s_x2 = sem("s_x2")
        s_st2 = sem("s_st2")
        s_nm2 = sem("s_nm2")
        s_ln2 = sem("s_ln2")
        s_rs2 = sem("s_rs2")
        s_x2n = sem("s_x2n")
        s_x2Tp = sem("s_x2Tp")
        s_x2nT = sem("s_x2nT")
        s_xr = sem("s_xr")
        s_lg = sem("s_lg")
        s_rt = sem("s_rt")
        s_lexp = sem("s_lexp")
        s_rank = sem("s_rank")
        s_pos = sem("s_pos")
        s_send = [sem(f"s_send{i}") for i in range(2)]
        s_pads = sem("s_pads")
        s_total = sem("s_total")
        s_plan = sem("s_plan")
        s_w1h = sem("s_w1h")
        s_w1l = sem("s_w1l")
        f_load = [sem(f"f_load{i}") for i in range(RING)]
        f_xT = sem("f_xT")
        f_xh = sem("f_xh")
        f_xl = sem("f_xl")
        f_up = sem("f_up")
        f_gelu = sem("f_gelu")
        f_hT = sem("f_hT")
        f_hTs = sem("f_hTs")
        f_down = sem("f_down")
        f_y = sem("f_y")
        f_send = [sem(f"f_send{i}") for i in range(RING)]
        f_settled = sem("f_settled")
        s_yb = [sem(f"s_yb{i}") for i in range(GROUPS)]
        s_y1 = sem("s_y1")
        s_y2 = sem("s_y2")
        s_out = sem("s_out")

        ROUTE = 23
        SELECTED = 18
        STATS = 2 * GROUP
        POS = 5
        SEND = 16 * 2 * GROUP
        PLAN = 16
        PAD_ROWS = 3

        x_v = x.rearrange("b t d -> t b d")
        out_v = out.rearrange("b t d -> t b d")
        picked_v = picked.rearrange("(b t k) d -> t b k d", t=T, k=2)
        mask_v = mask.rearrange("b t -> (b t)").unsqueeze(0)
        M0 = 2 * GROUP * T
        ROWS = (slice(0, 64), slice(64, 128))
        OTHER = (64, 0)

        def flat(ap):
            return ap.rearrange("p a b -> p (a b)")

        def heads(ap):
            return ap.rearrange("p (h s) -> p h s", h=HALF)

        def seqs(ap):
            return ap.rearrange("p (b s) -> p b s", b=GROUP)

        block = stack.enter_context(nc.Block())

        @block.sync
        def _(sp):
            def row_of(at, highest):
                return nc.values_load(
                    at, engines=[mybir.EngineType.SP], min_val=0, max_val=highest,
                    skip_runtime_bounds_check_because="no expert has more than CAP rows, and no "
                    "slot past an expert's last one starts behind SPARE slots of zeros")

            sp.dma_start(xs[:, 0:GROUP, :], x_v[:, 0:GROUP, :]).then_inc(s_x, 16)
            sp.dma_start(ident[:, :], ident_c).then_inc(s_ident, 16)
            sp.dma_start(wts[:, :], weights).then_inc(s_wts, 16)
            sp.dma_start(vecs[:, :], vectors.broadcast_to([128, D + 2])).then_inc(s_wts, 16)
            for b in range(2):
                sp.dma_start(ctxs[:, b, :, :], ctxT[:, b, :, :]).then_inc(s_ctx[b], 16)
            sp.dma_start(maskbc[:, 0:M0], mask_v[:, 0:M0].broadcast_to([128, M0])).then_inc(s_mask0, 16)
            sp.dma_start(tables[:, :], tables_c).then_inc(s_tables, 16)
            sp.dma_start(maskrow[:, :], mask_v).then_inc(s_tables, 16)
            for b in range(2, GROUP):
                sp.dma_start(ctxs[:, b, :, :], ctxT[:, b, :, :]).then_inc(s_ctx[b], 16)
            sp.wait_ge(s_x, 16)
            sp.dma_start(xs[:, GROUP:2 * GROUP, :], x_v[:, GROUP:2 * GROUP, :]).then_inc(s_x, 16)
            sp.dma_start(integers[:, :], integers_c).then_inc(s_ints, 16)
            def penalise(n, r):
                sp.wait_ge(s_kb, n + 1)
                for h in range(2):
                    sp.dma_start(kblk[OTHER[h]:OTHER[h] + 1, r, HALF * h:HALF * (h + 1), :],
                                 maskrow[:, bass.ds(T * n, T)].unsqueeze(1).broadcast_to([1, HALF, T])
                                 ).then_inc(s_penal[r], 16)

            def loads(g, more=True, experts=False):
                if more:
                    sp.wait_ge(s_x, 16 * (g + 1))
                    sp.dma_start(xs[:, bass.ds(GROUP * (g + 1), GROUP), :],
                                 x_v[:, bass.ds(GROUP * (g + 1), GROUP), :]).then_inc(s_x, 16)
                    wait(sp, s_mask, 16 * (g - 1))
                    sp.dma_start(maskbc[:, bass.ds(GROUP * T * (g + 1), GROUP * T)],
                                 mask_v[:, bass.ds(GROUP * T * (g + 1), GROUP * T)]
                                 .broadcast_to([128, GROUP * T])).then_inc(s_mask, 16)
                for b in range(GROUP):
                    sp.wait_ge(s_proj, GROUP * g + (b - GROUP + 1))
                    sp.dma_start(ctxs[:, b, :, :],
                                 ctxT[:, bass.ds(GROUP * g + b, 1), :, :]
                                 .rearrange("p o c t -> p (o c) t")).then_inc(s_ctx[b], 16)
                    penalise(GROUP * (g - 1) + b, b % 2)
                    if experts:
                        e = EXPERTS // GROUP * b
                        sp.dma_start(w1s[:, e:e + EXPERTS // GROUP, :],
                                     w1[e:e + EXPERTS // GROUP, :, :].rearrange("e d h -> d e h")
                                     ).then_inc(s_w1, 16)

            sp.wait_ge(s_pen, 1)
            loads(1)
            loads(2, experts=True)
            with sp.Fori(3, GROUPS - 1) as g:
                loads(g)
            loads(GROUPS - 1, more=False)
            for b in range(GROUP):
                penalise(GROUP * (GROUPS - 1) + b, b % 2)
            for e in range(EXPERTS):
                sp.dma_start(w2s[:, e, :, :], w2[e, :, :].rearrange("(c p) d -> p c d", p=128)
                             ).then_inc(s_ffnw, 16)
            sp.wait_ge(s_pad0, 2)
            sp.dma_start(rows[EXPERTS * REGION:EXPERTS * REGION + 128 * SPARE, :]
                         .rearrange("(i p) c -> p i c", p=128),
                         padrow[:, :].unsqueeze(1).broadcast_to([128, SPARE, ROW])).then_inc(s_pads, 16)
            sp.wait_ge(s_plan, PAD_ROWS)
            for e in range(EXPERTS):
                r = row_of(pad_row[0:1, e:e + 1], EXPERTS * REGION - 128)
                sp.dma_start(rows[bass.ds(r, 128), :], padrow[:, :]).then_inc(s_pads, 16)
            sp.wait_ge(s_plan, PLAN)
            first = [row_of(slot_row[0:1, r:r + 1], (EXPERTS + 1) * REGION - 128) for r in range(RING)]
            sp.wait_ge(s_pads, 16 * (1 + EXPERTS))
            for i, used in (outbox(GROUPS - 2), outbox(GROUPS - 1)):
                sp.wait_ge(s_send[i], SEND * (used + 1))
            for r in range(RING):
                sp.dma_start(xg[:, r, :], rows[bass.ds(first[r], 128), :]).then_inc(f_load[r], 16)

            def load(j, r):
                at = row_of(slot_row[0:1, j:j + 1] if isinstance(j, int)
                            else slot_row[0:1, bass.ds(j, 1)], (EXPERTS + 1) * REGION - 128)
                sp.wait_ge(f_send[r], 2 * (j - r))
                sp.dma_start(xg[:, r, :], rows[bass.ds(at, 128), :]).then_inc(f_load[r], 16)

            with sp.Fori(1, SLOTS // RING) as q:
                for r in range(RING):
                    load(RING * q + r, r)
            for j in range(SLOTS // RING * RING, SLOTS):
                load(j, j % RING)
            for r in range(RING):
                sp.wait_ge(f_send[r], 16 * len(range(r, SLOTS, RING)))
            for G in range(GROUPS):
                sp.dma_start(yb[G], picked_v[:, GROUP * G:GROUP * (G + 1), :, :]).then_inc(s_yb[G], 16)
            sp.wait_ge(s_out, 16 * GROUPS)

        @block.gpsimd
        def _(pool):
            nc.gpsimd.memset(minus_half[:, :], -0.5).then_inc(s_zero, 1)
            nc.gpsimd.memset(qT[:, :, :, :], 0.0).then_inc(s_zero, 1)
            nc.gpsimd.memset(vals[:, :, :, :], 0.0).then_inc(s_zero, 1)
            pool.wait_ge(s_zero, 3)
            nc.gpsimd.memset(vals[:, :, :, HD:HD + 1], 1.0).then_inc(s_pool0, 1)

            def step(g, k):
                G = group(g, 0)
                if k == 1 and G is not None:
                    pool.wait_ge(s_ln1, G + 1)
                    wait(pool, s_xn, GROUP * G)
                    nc.gpsimd.tensor_tensor(rs1[:, :], ve1[:, :], minus_half[:, :],
                                            ALU.pow).then_inc(s_rs1, 1)
                    pool.wait_ge(s_rs1, G + 1)
                    pool.wait_ge(s_nm1, G + 1)
                    nc.gpsimd.tensor_tensor(mr1[:, :], nm1[:, :], rs1[:, :], ALU.mult).then_inc(s_mr1, 1)
                G = group(g, LAG_OUT)
                if k == 2 and G is not None:
                    pool.wait_ge(s_ln2, G + 1)
                    wait(pool, s_x2n, GROUP * G)
                    nc.gpsimd.tensor_tensor(rs2[:, :], ve2[:, :], minus_half[:, :],
                                            ALU.pow).then_inc(s_rs2, 1)
                n = sequence(g, k, LAG_PROJ)
                if n is not None:
                    r = (k - LAG_PROJ) % 2
                    pool.wait_ge(s_k, n + 1)
                    wait(pool, s_sc, 2 * (n - 1))
                    nc.gpsimd.tensor_tensor(
                        kblk[:, r, :, :], kT[:, r, :].unsqueeze(1).broadcast_to([128, HEADS, T]),
                        headmask.unsqueeze(2).broadcast_to([128, HEADS, T]),
                        ALU.mult).then_inc(s_kb, 1)
                G = group(g, LAG_SEND)
                if SENDS[k] and G is not None:
                    i = outbox(G)[0]
                    pool.wait_ge(s_pos, POS * G + POS)
                    pool.wait_ge(s_rt, ROUTE * G + ROUTE)
                    pool.wait_ge(s_xr, 2 * G + 2)
                    settled()
                    for t in SENDS[k]:
                        pick, b = divmod(t, GROUP)
                        nc.gpsimd.indirect_dma_start(
                            out=rows, out_offset=bass.IndirectOffsetOnAxis(
                                ap=posi[:, i, pick, b:b + 1], axis=0),
                            in_=xr[:, i, pick, b, :], in_offset=None).then_inc(s_send[i], 16)
                G = group(g, 0)
                if k == 3 and G is not None:
                    if isinstance(g, int) and g == 0:
                        pool.wait_ge(s_setup, 3)
                        pool.wait_ge(s_tables, 32)
                    pool.wait_ge(s_xn, GROUP * G + GROUP)
                    nc.gpsimd.tensor_tensor(
                        xs[:, bass.ds(GROUP * G, GROUP), :], xs[:, bass.ds(GROUP * G, GROUP), :],
                        bout_g[:, :].unsqueeze(1).broadcast_to([128, GROUP, D]),
                        ALU.add).then_inc(s_xb, 1)

            bound = pool.to_reg(PICKS - 1)
            carriers = []

            def settled():
                carriers.append(None)
                c = len(carriers) % 32
                return nc.gpsimd.tensor_tensor(pscratch[0:1, c:c + 1], minus_half[0:1, 0:1],
                                               minus_half[0:1, 0:1], ALU.add)

            each_step(pool, step)

            def send(j, r):
                pool.wait_ge(f_y, j + 1)
                wait(pool, f_settled, j)
                settled().then_inc(f_settled, 1)
                nc.gpsimd.indirect_dma_start(
                    out=picked, out_offset=bass.IndirectOffsetOnAxis(
                        ap=xg[:, r, D + 1:D + 2].bitcast(I32), axis=0),
                    in_=yo[:, r, :], in_offset=None, bounds_check=bound,
                    oob_is_err=False).then_inc(f_send[r], 16)

            for r in range(RING):
                send(r, r)
            with pool.Fori(1, SLOTS // RING) as q:
                for r in range(RING):
                    send(RING * q + r, r)
            for j in range(SLOTS // RING * RING, SLOTS):
                send(j, j % RING)

        @block.scalar
        def _(act):
            act.wait_ge(s_wts, 32)
            nc.scalar.activation(tgates[:, :], gates, ACT.Tanh).then_inc(s_gate, 1)

            def normalise(G, seqs_of):
                for b in seqs_of:
                    nc.scalar.activation(
                        xn[:, b, :], xs[:, bass.ds(GROUP * G + b, 1), :].rearrange("p o d -> p (o d)"),
                        ACT.Identity, bias=mr1[:, b:b + 1], scale=rs1[:, b:b + 1]).then_inc(s_xn, 1)

            def step(g, k):
                n = sequence(g, k, LAG_PROJ)
                if n is not None:
                    act.wait_ge(s_xT, n + 1)
                    wait(act, s_proj, n - 1)
                    nc.scalar.activation(xnT[:, (k - LAG_PROJ) % 2, :], ps_xT[:, 0:T],
                                         ACT.Copy).then_inc(s_xnT, 1)
                n = sequence(g, k, LAG_PV)
                if n is not None:
                    r = (k - LAG_PV) % 2
                    wait(act, s_pv, n - 1)
                    for h in range(2):
                        act.wait_ge(s_pT, 2 * n + (h + 1))
                        nc.scalar.activation(flat(probT[:, r, HALF * h:HALF * (h + 1), :]),
                                             ps_pT[h][:, :], ACT.Copy).then_inc(s_pTs, 1)
                G = group(g, LAG_OUT)
                if k == 0 and G is not None:
                    act.wait_ge(s_onTp, G + 1)
                    wait(act, s_oproj, G)
                    nc.scalar.activation(flat(onT[:, :, :]), ps_tail[:, :], ACT.Copy).then_inc(s_onT, 1)
                n = sequence(g, k, LAG_PROJ)
                if n is not None:
                    act.wait_ge(s_proj, n + 1)
                    wait(act, s_kb, n - 1)
                    nc.scalar.activation(kT[:, (k - LAG_PROJ) % 2, :], ps_proj[:, 0:T], ACT.Identity,
                                         bias=bkey).then_inc(s_k, 1)
                    wait(act, s_pv, n - 3)
                    nc.scalar.activation(
                        vals[:, (k - LAG_PROJ) % 4, :, 0:HD],
                        ps_proj[:, 2 * T:3 * T].rearrange("p (h c) -> p h c", c=HD),
                        ACT.Copy).then_inc(s_v, 1)
                n = sequence(g, k, LAG_SCORE)
                if n is not None:
                    r = (k - LAG_SCORE) % 2
                    for h in range(2):
                        act.wait_ge(s_cen, 2 * n + (h + 1))
                        p = prob[:, r, HALF * h:HALF * (h + 1), :]
                        if h == 1 and k in LATE_MAX:
                            wait(act, s_pT, 2 * (n - 1))
                            for j in range(HALF):
                                last = nc.scalar.activation(
                                    p[:, j, :], ps_score[1][:, j * T:(j + 1) * T], ACT.Exp,
                                    scale=SCALE, bias=nmax[:, r, j:j + 1])
                        else:
                            last = nc.scalar.activation(flat(p), flat(p), ACT.Exp, scale=SCALE)
                        last.then_inc(s_exp, 1)
                G = group(g, LAG_ROUTE)
                if k == 0 and G is not None:
                    act.wait_ge(s_x2Tp, G + 1)
                    wait(act, s_lg, G)
                    nc.scalar.activation(flat(x2nT[:, :, :]), ps_tail[:, :],
                                         ACT.Copy).then_inc(s_x2nT, 1)
                n = sequence(g, k, LAG_PV)
                if n is not None:
                    act.wait_ge(s_pv, n + 1)
                    wait(act, s_o, n)
                    nc.scalar.activation(flat(oT[:, :, :]), ps_o[:, 0:2 * T], ACT.Copy).then_inc(s_oT, 1)
                G = group(g, LAG_ROUTE)
                if k == 2 and G is not None:
                    act.wait_ge(s_rt, ROUTE * G + 2)
                    nc.scalar.activation(flat(lexp[:, :, :]), flat(lcen[:, :, :]),
                                         ACT.Exp).then_inc(s_lexp, 1)
                G = group(g, LAG_ROUTE)
                if k == 3 and G is not None:
                    box, used = outbox(G)
                    wait(act, s_send[box], SEND * used)
                    for i in range(2):
                        nc.scalar.activation(xr[:, box, i, :, 0:D], x2n[:, :, :],
                                             ACT.Copy).then_inc(s_xr, 1)
                G = group(g, 0)
                if k == 2 and G is not None:
                    act.wait_ge(s_mr1, G + 1)
                    wait(act, s_xT, GROUP * (G - 1) + 3)
                    normalise(G, range(3))
                if k == 3 and G is not None:
                    wait(act, s_xT, GROUP * G)
                    normalise(G, range(3, GROUP))

            each_step(act, step)
            act.wait_ge(s_w1, 16 * GROUP)
            for e in range(EXPERTS):
                nc.scalar.activation(w1h[:, e, :], w1s[:, e, :], ACT.Copy).then_inc(s_w1h, 1)
            nc.scalar.activation(ascratch[:, :], tgates[:, :], ACT.Gelu)

            def work(q, r):
                j = slot_of(q, r, 0)
                if j is not None:
                    act.wait_ge(f_xT, j + 1)
                    wait(act, f_up, j - XRING + 1)
                    nc.scalar.activation(xh[:, r % XRING, :], ps_x[r % 2][:, 0:128],
                                         ACT.Copy).then_inc(f_xh, 1)
                j = slot_of(q, r, LAG_UP)
                if j is not None:
                    i = (r - LAG_UP) % 2
                    act.wait_ge(f_up, j + 1)
                    wait(act, f_hT, j - 1)
                    nc.scalar.activation(hid[:, i, :, :], heads(ps_score[i][:, :]),
                                         ACT.Gelu).then_inc(f_gelu, 1)

            each_slot(act, work)
            for G in range(GROUPS):
                act.wait_ge(s_y2, G + 1)
                act.dma_start(out_v[:, GROUP * G:GROUP * (G + 1), :],
                              xs[:, GROUP * G:GROUP * (G + 1), :]).then_inc(s_out, 16)

        @block.vector
        def _(dve):
            carriers = []

            def settled():
                carriers.append(None)
                c = len(carriers) % 32
                nc.vector.memset(scratch[:, c:c + 1], 0.0)

            def statistics(G, s, st, mv, ve, nm, done, used):
                wait(dve, used, GROUP * G)
                settled()
                for b in range(GROUP):
                    nc.vector.bn_stats(st[:, b, :], xs[:, bass.ds(GROUP * G + b, 1), :]
                                       .rearrange("p o d -> p (o d)")).then_inc(s, 1)
                dve.wait_ge(s, STATS * G + GROUP)
                settled()
                for b in range(GROUP):
                    nc.vector.bn_aggr(mv[:, b, :], st[:, b, :]).then_inc(s, 1)
                dve.wait_ge(s, STATS * G + STATS)
                nc.vector.tensor_scalar(nm[:, :], mv[:, :, 0], -1.0, None, ALU.mult).then_inc(done[0], 1)
                nc.vector.tensor_scalar(ve[:, :], mv[:, :, 1], EPS, None, ALU.add).then_inc(done[1], 1)

            def early_setup():
                dve.wait_ge(s_gate, 1)
                nc.vector.tensor_scalar(flat(wout_g[:, :, :]), wout, tgates[:, 0:1], None,
                                        ALU.mult).then_inc(s_setup, 1)
                nc.vector.tensor_scalar(bout_g[:, :], bout, tgates[:, 0:1], None,
                                        ALU.mult).then_inc(s_setup, 1)
                dve.wait_ge(s_zero, 3)
                nc.vector.memset(qT[OTHER[0]:OTHER[0] + 1, :, 0, :], 1.0).then_inc(s_ones, 1)
                nc.vector.memset(qT[OTHER[1]:OTHER[1] + 1, :, 1, :], 1.0).then_inc(s_ones, 1)
                dve.wait_ge(s_bias, 1)
                dve.wait_ge(s_setup, 2)
                nc.vector.tensor_tensor(bout_g[:, :], bout_g[:, :], ps_tail[:, 0:D],
                                        ALU.add).then_inc(s_setup, 1)
                dve.wait_ge(s_tables, 32)
                nc.vector.tensor_scalar(maskrow[:, :], maskrow[:, :], -1.0, MASKED,
                                        ALU.add, ALU.mult).then_inc(s_pen, 1)

            def late_setup():
                nc.vector.memset(padrow[:, 0:D], 0.0).then_inc(s_pad0, 1)
                nc.vector.memset(before[:, :], 0.0).then_inc(s_late, 1)
                nc.vector.memset(ones_b[:, :], 1.0).then_inc(s_late, 1)
                nc.vector.memset(rsum[:, :, :], 1.0).then_inc(s_late, 1)
                dve.wait_ge(s_tables, 32)
                dve.wait_ge(s_ints, 16)
                nc.vector.tensor_copy(padrow[:, D:ROW].bitcast(I32), padmeta).then_inc(s_pad0, 1)
                nc.vector.tensor_copy(strict_b[:, :], strict).then_inc(s_late, 1)
                nc.vector.tensor_scalar(regions[:, :], iota8, float(REGION), None, ALU.mult).then_inc(s_late, 1)
                dve.wait_ge(s_late, 5)
                settled()

            def routing(G):
                at = [0]

                def then(ins):
                    at[0] += 1
                    ins.then_inc(s_rt, 1)

                def done(count):
                    dve.wait_ge(s_rt, ROUTE * G + count)

                def per_expert(ap):
                    return ap.unsqueeze(2).broadcast_to([128, GROUP, EXPERTS])

                def first():
                    logits = seqs(ps_tail[:, :])[:, :, 0:EXPERTS]
                    dve.wait_ge(s_lg, G + 1)
                    then(nc.vector.tensor_reduce(lmax[:, :], logits, AX.X, ALU.max))
                    done(1)
                    then(nc.vector.tensor_tensor(lcen[:, :, :], logits, per_expert(lmax[:, :]),
                                                 ALU.subtract))
                    dve.wait_ge(s_lexp, G + 1)
                    settled()
                    for b in range(GROUP):
                        then(nc.vector.max(top[:, b, :], lexp[:, b, :]))
                    then(nc.vector.tensor_reduce(lsum[:, :], lexp[:, :, :], AX.X, ALU.add))
                    done(6)
                    settled()
                    for b in range(GROUP):
                        then(nc.vector.max_index(topi[:, b, :], top[:, b, :], lexp[:, b, :]))
                    done(7)
                    then(nc.vector.reciprocal(linv[:, :], lsum[:, :]))
                    done(11)
                    then(nc.vector.tensor_copy(topf[:, :, :], topi[:, :, :]))
                    done(12)
                    then(nc.vector.tensor_tensor(topp[:, :, :], top[:, :, 0:2],
                                                 linv[:, :].unsqueeze(2).broadcast_to([128, GROUP, 2]),
                                                 ALU.mult))

                def second():
                    assert at[0] == 14
                    experts = iota8.unsqueeze(1).broadcast_to([128, GROUP, EXPERTS])
                    done(14)
                    wait(dve, s_pos, POS * G)
                    for i in range(2):
                        then(nc.vector.tensor_tensor(sel[:, i, :, :], experts, per_expert(topf[:, :, i]),
                                                     ALU.is_equal))
                    then(nc.vector.scalar_tensor_tensor(tsum[:, :], topp[:, :, 0], 1e-9, topp[:, :, 1],
                                                        ALU.add, ALU.add))
                    done(16)
                    then(nc.vector.tensor_tensor(sel_b[:, :, :], sel[:, 0, :, :], sel[:, 1, :, :],
                                                 ALU.add))
                    assert at[0] == SELECTED

                def third():
                    done(17)
                    then(nc.vector.reciprocal(tinv[:, :], tsum[:, :]))
                    done(18)
                    then(nc.vector.tensor_reduce(picks[:, :], sel_b[:, :, :].rearrange("p b e -> p e b"),
                                                 AX.X, ALU.add))
                    done(19)
                    then(nc.vector.tensor_scalar(tw[:, :], tinv[:, :], tgates[:, 1:2], None, ALU.mult))
                    done(21)
                    assert at[0] == 21

                return first, second, third

            def label(G):
                box, used = outbox(G)
                wait(dve, s_send[box], SEND * used)
                nc.vector.tensor_copy(
                    xr[:, box, :, :, D + 1].bitcast(I32),
                    dest[:, bass.ds(GROUP * G, GROUP), :].rearrange("p b k -> p k b")).then_inc(s_rt, 1)
                dve.wait_ge(s_rt, ROUTE * G + 21)
                nc.vector.tensor_tensor(
                    xr[:, box, :, :, D].rearrange("p k b -> p b k"), topp[:, :, :],
                    tw[:, :].unsqueeze(2).broadcast_to([128, GROUP, 2]), ALU.mult).then_inc(s_rt, 1)
                dve.wait_ge(s_rt, ROUTE * G + ROUTE)

            def place_picks(G):
                dve.wait_ge(s_rank, G + 1)
                nc.vector.tensor_tensor(
                    place[:, :, :], ps_tail[:, 0:GROUP * EXPERTS].rearrange("p (b e) -> p b e", b=GROUP),
                    regions[:, :].unsqueeze(1).broadcast_to([128, GROUP, EXPERTS]),
                    ALU.add).then_inc(s_pos, 1)

            def position(G):
                dve.wait_ge(s_pos, POS * G + 1)
                nc.vector.tensor_tensor(
                    placed[:, :, :, :], sel[:, :, :, :],
                    place[:, :, :].unsqueeze(1).broadcast_to([128, 2, GROUP, EXPERTS]),
                    ALU.mult).then_inc(s_pos, 1)
                nc.vector.tensor_tensor(before[:, :], before[:, :], picks[:, :], ALU.add).then_inc(s_pos, 1)
                dve.wait_ge(s_pos, POS * G + 2)
                nc.vector.tensor_reduce(pos[:, :, :], placed[:, :, :, :], AX.X, ALU.add).then_inc(s_pos, 1)
                box, used = outbox(G)
                wait(dve, s_send[box], SEND * used)
                dve.wait_ge(s_pos, POS * G + 4)
                nc.vector.tensor_copy(posi[:, box, :, :], pos[:, :, :]).then_inc(s_pos, 1)

            def plan():
                at = [0]

                def then(ins):
                    at[0] += 1
                    ins.then_inc(s_plan, 1)
                    dve.wait_ge(s_plan, at[0])

                dve.wait_ge(s_total, 1)
                then(nc.vector.tensor_copy(total[:, :], ps_tail[:, 0:EXPERTS]))
                then(nc.vector.tensor_tensor(prow[:, :], total[:, :], regions[:, :], ALU.add))
                then(nc.vector.tensor_copy(pad_row[:, :], prow[:, :]))
                then(nc.vector.tensor_scalar(srow[:, 0:BATCH], iota[:, 0:BATCH], 128.0, None, ALU.mult))
                then(nc.vector.tensor_tensor(
                    more[:, :, :], total[:, :].unsqueeze(2).broadcast_to([128, EXPERTS, BATCH]),
                    srow[:, 0:BATCH].unsqueeze(1).broadcast_to([128, EXPERTS, BATCH]), ALU.is_gt))
                then(nc.vector.tensor_reduce(nslots[:, :], more[:, :, :], AX.X, ALU.add))
                then(nc.vector.tensor_tensor(
                    upto[:, :, :], below,
                    nslots[:, :].unsqueeze(1).broadcast_to([128, EXPERTS, EXPERTS]), ALU.mult))
                then(nc.vector.tensor_reduce(ends[:, :], upto[:, :, :], AX.X, ALU.add))
                then(nc.vector.tensor_tensor(
                    past[:, :, :], iota[:, 0:SLOTS].unsqueeze(2).broadcast_to([128, SLOTS, EXPERTS]),
                    ends[:, :].unsqueeze(1).broadcast_to([128, SLOTS, EXPERTS]), ALU.is_ge))
                then(nc.vector.tensor_tensor(
                    gone[:, :, :], past[:, :, :],
                    nslots[:, :].unsqueeze(1).broadcast_to([128, SLOTS, EXPERTS]), ALU.mult))
                then(nc.vector.tensor_reduce(sexp[:, :], past[:, :, :], AX.X, ALU.add))
                then(nc.vector.tensor_reduce(sgone[:, :], gone[:, :, :], AX.X, ALU.add))
                then(nc.vector.tensor_tensor(srow[:, :], iota[:, 0:SLOTS], sgone[:, :], ALU.subtract))
                then(nc.vector.tensor_scalar(sgone[:, :], srow[:, :], 128.0, None, ALU.mult))
                then(nc.vector.scalar_tensor_tensor(slot_row[:, :], sexp[:, :], float(REGION),
                                                    sgone[:, :], ALU.mult, ALU.add))
                then(nc.vector.tensor_scalar(slot_exp[:, :], sexp[:, :], float(EXPERTS - 1), None,
                                             ALU.min))
                assert at[0] == PLAN

            parts = []

            def step(g, k):
                n = sequence(g, k, LAG_SCORE)
                if n is not None:
                    r = (k - LAG_SCORE) % 2
                    wait(dve, s_cen, 2 * (n - 1))
                    for h in range(2):
                        dve.wait_ge(s_sc, 2 * n + (h + 1))
                        nc.vector.tensor_reduce(rowmax[:, r, HALF * h:HALF * (h + 1)],
                                                heads(ps_score[h][:, :]), AX.X, ALU.max
                                                ).then_inc(s_max, 1)
                n = sequence(g, k, LAG_O)
                if n is not None:
                    r = (k - LAG_O) % 2
                    o3 = ps_o[:, 0:2 * T].rearrange("p (h c) -> p h c", c=VPAD)
                    dve.wait_ge(s_o, n + 1)
                    wait(dve, s_on, n - 1)
                    nc.vector.reciprocal(rsum[:, r, :], o3[:, :, HD]).then_inc(s_rsum, 1)
                    dve.wait_ge(s_rsum, n + 1)
                    wait(dve, s_onTp, g - LAG_O // GROUP)
                    nc.vector.tensor_tensor(
                        on[:, (k - LAG_O) % GROUP, :].rearrange("p (h c) -> p h c", c=HD),
                        o3[:, :, 0:HD], rsum[:, r, :].unsqueeze(2).broadcast_to([128, HEADS, HD]),
                        ALU.mult).then_inc(s_on, 1)
                if k == 3 and group(g, LAG_ROUTE) is not None:
                    parts[1]()
                n = sequence(g, k, LAG_SCORE)
                if n is not None:
                    r = (k - LAG_SCORE) % 2
                    wait(dve, s_pT, 2 * (n - 1))
                    for h in range(2):
                        dve.wait_ge(s_max, 2 * n + (h + 1))
                        if h == 1 and k in LATE_MAX:
                            wait(dve, s_exp, 2 * (n - 1))
                            nc.vector.tensor_scalar(nmax[:, r, :], rowmax[:, r, HALF:HEADS], -SCALE,
                                                    None, ALU.mult).then_inc(s_cen, 1)
                        else:
                            nc.vector.tensor_tensor(
                                prob[:, r, HALF * h:HALF * (h + 1), :], heads(ps_score[h][:, :]),
                                rowmax[:, r, HALF * h:HALF * (h + 1)].unsqueeze(2)
                                .broadcast_to([128, HALF, T]), ALU.subtract).then_inc(s_cen, 1)
                if k == 3 and group(g, LAG_ROUTE) is not None:
                    parts[2]()
                n = sequence(g, k, LAG_PROJ)
                if n is not None:
                    r = (k - LAG_PROJ) % 2
                    cols = bass.ds(n * T, T)
                    if isinstance(n, int) and n == 0:
                        dve.wait_ge(s_mask0, 16)
                    if k == 0:
                        wait(dve, s_mask, 16 * (g - 2))
                    dve.wait_ge(s_v, n + 1)
                    wait(dve, s_sc, 2 * (n - 1))
                    for h, rows_of in enumerate(ROWS):
                        nc.vector.scalar_tensor_tensor(
                            qT[rows_of, r, h, :], ps_proj[rows_of, T:2 * T], bqry[rows_of, :],
                            maskbc[rows_of, cols], ALU.add, ALU.mult).then_inc(s_q, 1)
                    dve.wait_ge(s_xb, g)
                    x1 = xs[:, bass.ds(n, 1), :].rearrange("p o d -> p (o d)")
                    nc.vector.tensor_tensor(x1, ps_proj[:, 3 * T:4 * T], x1, ALU.add).then_inc(s_xo, 1)
                G = group(g, LAG_ROUTE)
                if k == 3 and G is not None:
                    place_picks(G)
                    label(G)
                    position(G)
                G = group(g, LAG_OUT)
                if k == 3 and G is not None:
                    dve.wait_ge(s_rs2, G + 1)
                    dve.wait_ge(s_nm2, G + 1)
                    wait(dve, s_x2Tp, G)
                    wait(dve, s_xr, 2 * G)
                    for b in range(GROUP):
                        nc.vector.tensor_scalar(
                            x2n[:, b, :],
                            xs[:, bass.ds(GROUP * G + b, 1), :].rearrange("p o d -> p (o d)"),
                            nm2[:, b:b + 1], rs2[:, b:b + 1], ALU.add, ALU.mult).then_inc(s_x2n, 1)
                G = group(g, 0)
                if k == 0 and G is not None:
                    dve.wait_ge(s_x, 16 * (G + 1))
                    statistics(G, s_st1, st1, mv1, ve1, nm1, (s_nm1, s_ln1), s_xn)
                G = group(g, LAG_OUT)
                if k == 1 and G is not None:
                    dve.wait_ge(s_oproj, G + 1)
                    wait(dve, s_xo, GROUP * G + GROUP)
                    x4 = xs[:, bass.ds(GROUP * G, GROUP), :]
                    nc.vector.tensor_tensor(x4, seqs(ps_tail[:, :]), x4, ALU.add).then_inc(s_x2, 1)
                    dve.wait_ge(s_x2, G + 1)
                    statistics(G, s_st2, st2, mv2, ve2, nm2, (s_nm2, s_ln2), s_x2n)
                G = group(g, LAG_ROUTE)
                if k == 2 and G is not None:
                    parts[:] = routing(G)
                    parts[0]()
                if isinstance(g, int) and (g, k) == (0, 1):
                    early_setup()
                if isinstance(g, int) and (g, k) == (1, 0):
                    late_setup()

            each_step(dve, step)
            plan()
            for e in range(EXPERTS):
                dve.wait_ge(s_w1h, e + 1)
                nc.vector.tensor_tensor(w1l[:, e, :], w1s[:, e, :], w1h[:, e, :].bitcast(F32),
                                        ALU.subtract).then_inc(s_w1l, 1)

            def work(q, r):
                j = slot_of(q, r, 0)
                if j is not None:
                    dve.wait_ge(f_xh, j + 1)
                    wait(dve, f_up, j - XRING + 1)
                    nc.vector.tensor_tensor(xl[:, r % XRING, :], ps_x[r % 2][:, 0:128],
                                            xh[:, r % XRING, :].bitcast(F32),
                                            ALU.subtract).then_inc(f_xl, 1)
                j = slot_of(q, r, LAG_HT)
                if j is not None:
                    i = (r - LAG_HT) % 2
                    dve.wait_ge(f_hT, j + 1)
                    wait(dve, f_down, j - 1)
                    nc.vector.tensor_copy(hidT[:, i, :, :], heads(ps_pT[i][:, :])).then_inc(f_hTs, 1)
                j = slot_of(q, r, LAG_DOWN)
                if j is not None:
                    i = (r - LAG_DOWN) % RING
                    dve.wait_ge(f_down, j + 1)
                    wait(dve, f_send[i], 2 * (j - i))
                    nc.vector.tensor_scalar(yo[:, i, :], ps_y[i % 2][:, 0:D], xg[:, i, D:D + 1], None,
                                            ALU.mult).then_inc(f_y, 1)

            each_slot(dve, work)

            for G in range(GROUPS):
                x4 = xs[:, GROUP * G:GROUP * (G + 1), :]
                dve.wait_ge(s_yb[G], 16)
                nc.vector.tensor_tensor(x4, x4, yb[G][:, :, 0, :], ALU.add).then_inc(s_y1, 1)
                dve.wait_ge(s_y1, G + 1)
                nc.vector.tensor_tensor(x4, x4, yb[G][:, :, 1, :], ALU.add).then_inc(s_y2, 1)

        @block.tensor
        def _(pe):
            pe.wait_ge(s_setup, 1)
            nc.tensor.matmul(ps_tail[:, 0:D], bval.broadcast_to([128, 128]), wout_g[:, 1, :],
                             start=True, stop=True).then_inc(s_bias, 1)
            pe.wait_ge(s_ident, 16)

            def step(g, k):
                n = sequence(g, k, LAG_PROJ)
                if n is not None:
                    pe.wait_ge(s_xn, n + 1)
                    wait(pe, s_xnT, n)
                    nc.tensor.transpose(ps_xT[:, 0:T], xn[:, (k - LAG_PROJ) % GROUP, :],
                                        ident[:, :]).then_inc(s_xT, 1)
                n = sequence(g, k, LAG_SCORE)
                if n is not None:
                    r = (k - LAG_SCORE) % 2
                    if isinstance(n, int) and n == 0:
                        pe.wait_ge(s_ones, 2)
                    pe.wait_ge(s_q, 2 * n + 2)
                    pe.wait_ge(s_penal[r], 16 * (n - r) + 32)
                    for h in range(2):
                        wait(pe, s_exp if h == 1 and (k - 1) % GROUP in LATE_MAX else s_cen,
                             2 * n + (h - 1))
                        nc.tensor.matmul(ps_score[h][:, :], qT[:, r, h, :],
                                         flat(kblk[:, r, HALF * h:HALF * (h + 1), :]),
                                         start=True, stop=True).then_inc(s_sc, 1)
                G = group(g, LAG_OUT)
                if k == 0 and G is not None:
                    pe.wait_ge(s_on, GROUP * G + GROUP)
                    wait(pe, s_pos, POS * (G - 2) + 1)
                    for b in range(GROUP):
                        last = nc.tensor.transpose(ps_tail[:, b * T:(b + 1) * T], on[:, b, :], ident[:, :])
                    last.then_inc(s_onTp, 1)
                n = sequence(g, k, LAG_O)
                if n is not None:
                    pe.wait_ge(s_oT, n + 1)
                    for h in range(2):
                        last = nc.tensor.transpose(ps_o[:, h * T:(h + 1) * T], oT[:, h, :], ident[:, :])
                    last.then_inc(s_o, 1)
                n = sequence(g, k, LAG_PV)
                if n is not None:
                    r = (k - LAG_PV) % 2
                    for h in range(2):
                        pe.wait_ge(s_exp, 2 * n + (h + 1))
                        wait(pe, s_pTs, 2 * n + (h - 1))
                        for j in range(HALF):
                            last = nc.tensor.transpose(ps_pT[h][:, j * T:(j + 1) * T],
                                                       prob[:, r, HALF * h + j, :], ident[:, :])
                        last.then_inc(s_pT, 1)
                n = sequence(g, k, LAG_PROJ)
                if n is not None:
                    r = (k - LAG_PROJ) % 2
                    b = (k - LAG_PROJ) % GROUP
                    pe.wait_ge(s_xnT, n + 1)
                    pe.wait_ge(s_ctx[b], 16 * g)
                    wait(pe, s_xo, n)
                    for c in range(FCH):
                        nc.tensor.matmul(ps_proj[:, 0:T], wsrc[:, c, 0:D], ctxs[:, b, c, :],
                                         start=(c == 0), stop=(c == FCH - 1))
                    nc.tensor.matmul(ps_proj[:, T:2 * T], wtgt, xnT[:, r, :], start=True, stop=True)
                    for c in range(FCH):
                        nc.tensor.matmul(ps_proj[:, 2 * T:3 * T], ctxs[:, b, c, :], wsrc[:, c, D:2 * D],
                                         start=(c == 0), stop=(c == FCH - 1))
                    nc.tensor.matmul(ps_proj[:, 3 * T:4 * T], xnT[:, r, :], wout_g[:, 0, :],
                                     start=True, stop=True).then_inc(s_proj, 1)
                G = group(g, LAG_ROUTE)
                if k == 0 and G is not None:
                    pe.wait_ge(s_x2n, GROUP * G + GROUP)
                    pe.wait_ge(s_onT, min(G + 2, GROUPS) if isinstance(G, int) else G + 2)
                    wait(pe, s_pos, POS * (G - 1) + 1)
                    for b in range(GROUP):
                        last = nc.tensor.transpose(ps_tail[:, b * T:(b + 1) * T], x2n[:, b, :], ident[:, :])
                    last.then_inc(s_x2Tp, 1)
                G = group(g, LAG_OUT)
                if k == 1 and G is not None:
                    pe.wait_ge(s_onT, G + 1)
                    wait(pe, s_x2nT, G)
                    for b in range(GROUP):
                        last = nc.tensor.matmul(ps_tail[:, b * D:(b + 1) * D], onT[:, b, :],
                                                wout_g[:, 1, :], start=True, stop=True)
                    last.then_inc(s_oproj, 1)
                G = group(g, LAG_ROUTE)
                if k == 2 and G is not None:
                    pe.wait_ge(s_x2nT, G + 1)
                    wait(pe, s_x2, min(G + 2, GROUPS) if isinstance(G, int) else G + 2)
                    wait(pe, s_pos, POS * (G - 1) + 1)
                    for b in range(GROUP):
                        last = nc.tensor.matmul(ps_tail[:, b * 128:(b + 1) * 128], x2nT[:, b, :],
                                                router, start=True, stop=True)
                    last.then_inc(s_lg, 1)
                n = sequence(g, k, LAG_PV)
                if n is not None:
                    r = (k - LAG_PV) % 2
                    if isinstance(n, int) and n == 0:
                        pe.wait_ge(s_pool0, 1)
                    pe.wait_ge(s_pTs, 2 * n + 2)
                    pe.wait_ge(s_v, n + 1)
                    wait(pe, s_on, n)
                    for h in range(HEADS):
                        q = h % HALF
                        last = nc.tensor.matmul(
                            ps_o[VPAD * q:VPAD * (q + 1), (h // HALF) * T:(h // HALF + 1) * T],
                            vals[:, (k - LAG_PV) % 4, h, :], probT[:, r, h, :], start=True, stop=True)
                    last.then_inc(s_pv, 1)
                G = group(g, LAG_ROUTE)
                if k == 3 and G is not None:
                    pe.wait_ge(s_rt, ROUTE * G + SELECTED)
                    if isinstance(G, int) and G == 0:
                        pe.wait_ge(s_late, 5)
                    nc.tensor.matmul(ps_tail[:, 0:GROUP * EXPERTS], strict_b[:, :], flat(sel_b[:, :, :]),
                                     start=True, stop=False)
                    for b in range(GROUP - 1):
                        left = GROUP - 1 - b
                        nc.tensor.matmul(
                            ps_tail[:, EXPERTS * (b + 1):EXPERTS * GROUP], ones_b[:, :],
                            sel_b[:, b, :].unsqueeze(1).broadcast_to([128, left, EXPERTS]),
                            start=False, stop=False)
                    nc.tensor.matmul(ps_tail[:, 0:GROUP * EXPERTS], ones_b[:, :],
                                     before[:, :].unsqueeze(1).broadcast_to([128, GROUP, EXPERTS]),
                                     start=False, stop=True).then_inc(s_rank, 1)

            each_step(pe, step)
            pe.wait_ge(s_pos, POS * GROUPS)
            nc.tensor.matmul(ps_tail[:, 0:EXPERTS], ones_b[:, :], before[:, :], start=True,
                             stop=True).then_inc(s_total, 1)

            pe.wait_ge(s_ffnw, 16 * EXPERTS)
            pe.wait_ge(s_w1l, EXPERTS)
            pe.wait_ge(s_plan, PLAN)

            def experts_of(first, count):
                at = (slot_exp[0:1, first:first + count] if isinstance(first, int)
                      else slot_exp[0:1, bass.ds(first, count)])
                _, values = nc.values_load_multi_w_load_instructions(
                    at, engines=[mybir.EngineType.PE], min_val=0, max_val=EXPERTS - 1,
                    skip_runtime_bounds_check_because="the plan takes the minimum with the last expert")
                return [bass.ds(v, 1) for v in values]

            turn = {}

            def work(q, r):
                if r == 0:
                    first = RING * q - LAG_DOWN if not isinstance(q, int) or q > 0 else 0
                    count = RING - LAG_UP + LAG_DOWN
                    if isinstance(q, int):
                        count = min(RING * q + RING - LAG_UP, SLOTS) - first
                    turn["experts"] = experts_of(first, count)
                    turn["first"] = 0 if isinstance(q, int) and q == 0 else -LAG_DOWN

                def expert(lag):
                    return turn["experts"][r - lag - turn["first"]]

                j = slot_of(q, r, 0)
                if j is not None:
                    pe.wait_ge(f_load[r], 2 * (j - r) + 16)
                    wait(pe, f_xl, j - 1)
                    nc.tensor.transpose(ps_x[r % 2][:, 0:128], xg[:, r, 0:D], ident[:, :]).then_inc(f_xT, 1)
                j = slot_of(q, r, LAG_UP)
                if j is not None:
                    i = (r - LAG_UP) % 2
                    e = expert(LAG_UP)
                    pe.wait_ge(f_xl, j + 1)
                    wait(pe, f_gelu, j - 1)
                    for a, w, first in ((xh, w1h, True), (xl, w1h, False), (xh, w1l, False)):
                        last = nc.tensor.matmul(ps_score[i][:, :], a[:, (r - LAG_UP) % XRING, :],
                                                w[:, e, :].rearrange("p o h -> p (o h)"),
                                                start=first, stop=(w is w1l))
                    last.then_inc(f_up, 1)
                j = slot_of(q, r, LAG_HT)
                if j is not None:
                    i = (r - LAG_HT) % 2
                    pe.wait_ge(f_gelu, j + 1)
                    wait(pe, f_hTs, j - 1)
                    for c in range(HCH):
                        last = nc.tensor.transpose(ps_pT[i][:, c * 128:(c + 1) * 128], hid[:, i, c, :],
                                                   ident[:, :])
                    last.then_inc(f_hT, 1)
                j = slot_of(q, r, LAG_DOWN)
                if j is not None:
                    i = (r - LAG_DOWN) % 2
                    e = expert(LAG_DOWN)
                    pe.wait_ge(f_hTs, j + 1)
                    wait(pe, f_y, j - 1)
                    for c in range(HCH):
                        last = nc.tensor.matmul(ps_y[i][:, 0:D], hidT[:, i, c, :],
                                                w2s[:, e, c, :].rearrange("p o d -> p (o d)"),
                                                start=(c == 0), stop=(c == HCH - 1))
                    last.then_inc(f_down, 1)

            each_slot(pe, work)


def kernel(x, ctx_2048, mask_BxS2_fk1, g_xattn, g_ffn, L0_xattn_W_src, L0_xattn_b_src,
           L0_xattn_W_tgt, L0_xattn_b_tgt, L0_xattn_W_out, L0_xattn_b_out, L0_ffn_router_w,
           L0_ffn_w1, L0_ffn_w2):
    import numpy as np
    import concourse.bacc as bacc
    from concourse.bass_utils import run_bass_kernel_spmd

    router = np.zeros((128, 128), np.float32)
    router[:, :EXPERTS] = np.asarray(L0_ffn_router_w).T
    ctx = np.asarray(ctx_2048)
    b_src, b_tgt, b_out = (np.asarray(a) for a in (L0_xattn_b_src, L0_xattn_b_tgt, L0_xattn_b_out))

    def chunks(a):
        return np.concatenate([a[:128], a[128:]], axis=1)

    dest = np.arange(PICKS, dtype=np.int32).reshape(BATCH, T, 2).transpose(1, 0, 2).reshape(T, -1)
    arrays = {
        "x": x, "ctxT": ctx.transpose(2, 0, 1).reshape(FCH, 128, BATCH, T).transpose(1, 2, 0, 3),
        "mask": mask_BxS2_fk1,
        "weights": np.concatenate([
            chunks(np.asarray(L0_xattn_W_src).T), np.asarray(L0_xattn_W_tgt).T,
            chunks(np.asarray(L0_xattn_W_out).T), router, b_src[:D, None], b_tgt[:, None],
            b_src[D:, None]], axis=1),
        "vectors": np.concatenate([b_out, np.asarray(g_xattn), np.asarray(g_ffn)])[None, :],
        "w1": L0_ffn_w1, "w2": L0_ffn_w2,
        "ident_c": np.eye(128, dtype=np.float32),
        "tables_c": np.concatenate([
            np.kron(np.eye(HEADS), np.ones((HD, 1))), np.tile(np.arange(SLOTS + EXPERTS), (128, 1)),
            np.triu(np.ones((128, 128)), 1),
            np.tile(np.tril(np.ones((EXPERTS, EXPERTS))).reshape(1, -1), (128, 1))],
            axis=1).astype(np.float32),
        "integers_c": np.concatenate([dest, np.tile(np.array([0, NOWHERE], np.int32), (128, 1))], axis=1),
    }
    nc = bacc.Bacc("TRN2", target_bir_lowering=False, num_devices=1)
    arrays = {k: np.ascontiguousarray(a) for k, a in arrays.items()}
    args = {k: nc.dram_tensor(k, a.shape, mybir.dt.from_np(a.dtype), kind="ExternalInput").ap()
            for k, a in arrays.items()}
    out = nc.dram_tensor("out", [BATCH, T, D], F32, kind="ExternalOutput").ap()
    rows = nc.dram_tensor("rows", [(EXPERTS + 1) * REGION, ROW], F32, kind="Internal").ap()
    picked = nc.dram_tensor("picked", [PICKS, D], F32, kind="Internal").ap()
    gated_cross_attention_moe(nc, out=out, rows=rows, picked=picked, **args)
    r = run_bass_kernel_spmd(nc, [arrays], core_ids=[0])
    return r.results[0]["out"]
```
